# Optimizing a Trainium2 kernel written in Bass

```python
import numpy as np
import jax
import jax.numpy as jnp

def _softmax(x, axis=-1):
    return jax.nn.softmax(x, axis=axis)

def _gelu(x):
    return jax.nn.gelu(x, approximate=True)

def _silu(x):
    return jax.nn.silu(x)

def _sigmoid(x):
    return jax.nn.sigmoid(x)

def _layernorm(x, axis=-1, eps=1e-05):
    m = jnp.mean(x, axis=axis, keepdims=True)
    v = jnp.var(x, axis=axis, keepdims=True)
    return (x - m) / jnp.sqrt(v + eps)

def _scatter_add(tgt, idx, src, axis=0):
    return tgt.at[idx].add(src)

def _segment_sum(src, seg, n):
    return jax.ops.segment_sum(src, seg, n)
kernel_name = 'mk_hybrid_d1_jaxref_r8_7be352'

def setup_inputs(seed: int=0):
    np.random.seed(seed)
    _w = jnp.asarray

    def _L0_attn_a_setup():
        import jax, jax.numpy as jnp
        import numpy as np
        HIDDEN = 256
        KEY = 256
        EPS = 1e-05
        key = jax.random.key(seed)
        k1, k2, k3 = jax.random.split(key, 3)
        B, S = (4, 256)
        x = jax.random.normal(k1, (B, S, HIDDEN), dtype=jnp.float32)
        bq = 1.0 / np.sqrt(HIDDEN)
        qkv = jax.random.uniform(k2, (HIDDEN, KEY * 3), minval=-bq, maxval=bq, dtype=jnp.float32)
        bo = 1.0 / np.sqrt(KEY)
        o_proj = jax.random.uniform(k3, (KEY, HIDDEN), minval=-bo, maxval=bo, dtype=jnp.float32)
        gamma = jnp.ones((HIDDEN,), dtype=jnp.float32)
        beta = jnp.zeros((HIDDEN,), dtype=jnp.float32)
        return {'x': x, 'qkv': qkv, 'o_proj': o_proj, 'gamma': gamma, 'beta': beta}
    _L0_attn_a_in = _L0_attn_a_setup()

    def _L0_attn_b_setup():
        import jax, jax.numpy as jnp
        import numpy as np
        T, B, H, N2 = (512, 2, 256, 8)

        def _s4d_kernel(log_dt, A_real_log, A_imag, C_re, C_im, L):
            dt = jnp.exp(log_dt)[:, None]
            A = -jnp.exp(A_real_log) + 1j * A_imag
            dtA = A * dt
            C = (C_re + 1j * C_im) * (jnp.exp(dtA) - 1.0) / A
            vander = jnp.exp(dtA[:, :, None] * jnp.arange(L))
            return 2.0 * jnp.einsum('hn,hnl->hl', C, vander).real
        key = jax.random.key(seed)
        k1, k2, k3, k4, k5 = jax.random.split(key, 5)
        x = jax.random.normal(k1, (T, B, H), dtype=jnp.float32)
        D_param = jax.random.normal(k2, (H,), dtype=jnp.float32)
        u = jax.random.uniform(k3, (H,), dtype=jnp.float32)
        log_dt = u * (jnp.log(0.1) - jnp.log(0.001)) + jnp.log(0.001)
        A_real_log = jnp.full((H, N2), jnp.log(0.5), dtype=jnp.float32)
        A_imag = jnp.broadcast_to(np.pi * jnp.arange(N2, dtype=jnp.float32), (H, N2))
        C_re = jax.random.normal(k4, (H, N2), dtype=jnp.float32)
        C_im = jax.random.normal(k5, (H, N2), dtype=jnp.float32)
        return {'x': x, 'D_param': D_param, 'log_dt': log_dt, 'A_real_log': A_real_log, 'A_imag': A_imag, 'C_re': C_re, 'C_im': C_im}
    _L0_attn_b_in = _L0_attn_b_setup()

    def _L0_ffn_setup():
        import jax, jax.numpy as jnp
        import numpy as np
        B, S, H, I = (1, 64, 256, 768)

        def _quantized_matmul(x, w, scale):
            wq = w.astype(jnp.float8_e4m3fn).astype(x.dtype)
            y = jnp.einsum('bsi,io->bso', x, wq)
            return y * scale
        key = jax.random.key(seed)
        ks = jax.random.split(key, 7)
        return {'x': jax.random.normal(ks[0], (B, S, H), dtype=jnp.float32), 'gate_w': jax.random.normal(ks[1], (H, I), dtype=jnp.float32) * 0.02, 'up_w': jax.random.normal(ks[2], (H, I), dtype=jnp.float32) * 0.02, 'down_w': jax.random.normal(ks[3], (I, H), dtype=jnp.float32) * 0.02, 'gate_scale': jax.random.uniform(ks[4], (I,), dtype=jnp.float32, minval=0.5, maxval=1.5), 'up_scale': jax.random.uniform(ks[5], (I,), dtype=jnp.float32, minval=0.5, maxval=1.5), 'down_scale': jax.random.uniform(ks[6], (H,), dtype=jnp.float32, minval=0.5, maxval=1.5)}
    _L0_ffn_in = _L0_ffn_setup()
    _d = {'L0_attn_a_x': _L0_attn_a_in['x'], 'L0_attn_a_qkv': _L0_attn_a_in['qkv'], 'L0_attn_a_o_proj': _L0_attn_a_in['o_proj'], 'L0_attn_a_gamma': _L0_attn_a_in['gamma'], 'L0_attn_a_beta': _L0_attn_a_in['beta'], 'L0_attn_b_D_param': _L0_attn_b_in['D_param'], 'L0_attn_b_log_dt': _L0_attn_b_in['log_dt'], 'L0_attn_b_A_real_log': _L0_attn_b_in['A_real_log'], 'L0_attn_b_A_imag': _L0_attn_b_in['A_imag'], 'L0_attn_b_C_re': _L0_attn_b_in['C_re'], 'L0_attn_b_C_im': _L0_attn_b_in['C_im'], 'L0_ffn_gate_w': _L0_ffn_in['gate_w'], 'L0_ffn_up_w': _L0_ffn_in['up_w'], 'L0_ffn_down_w': _L0_ffn_in['down_w'], 'L0_ffn_gate_scale': _L0_ffn_in['gate_scale'], 'L0_ffn_up_scale': _L0_ffn_in['up_scale'], 'L0_ffn_down_scale': _L0_ffn_in['down_scale']}
    _x0 = _d['L0_attn_a_x']
    _d['L0_attn_a_x'] = jax.random.normal(jax.random.fold_in(jax.random.key(seed), 1), (2, 512, 256), dtype=_x0.dtype)
    del _x0
    return _d

def reference(L0_attn_a_x, L0_attn_a_qkv, L0_attn_a_o_proj, L0_attn_a_gamma, L0_attn_a_beta, L0_attn_b_D_param, L0_attn_b_log_dt, L0_attn_b_A_real_log, L0_attn_b_A_imag, L0_attn_b_C_re, L0_attn_b_C_im, L0_ffn_gate_w, L0_ffn_up_w, L0_ffn_down_w, L0_ffn_gate_scale, L0_ffn_up_scale, L0_ffn_down_scale):

    def _L0_attn_a_ref(x, qkv, o_proj, gamma, beta):
        import jax, jax.numpy as jnp
        import numpy as np
        HIDDEN = 256
        KEY = 256
        EPS = 1e-05
        residual = x
        mu = jnp.mean(x, axis=-1, keepdims=True)
        var = jnp.mean((x - mu) ** 2, axis=-1, keepdims=True)
        x_norm = (x - mu) / jnp.sqrt(var + EPS) * gamma + beta
        q = x_norm @ qkv[:, :KEY]
        k = x_norm @ qkv[:, KEY:2 * KEY]
        v = x_norm @ qkv[:, 2 * KEY:]
        scale = 1.0 / jnp.sqrt(jnp.float32(KEY))
        scores = jnp.einsum('bsk,btk->bst', q, k) * scale
        S_len = x.shape[1]
        causal = jnp.tril(jnp.ones((S_len, S_len), dtype=bool))
        scores = jnp.where(causal[None], scores, -jnp.inf)
        attn = jax.nn.softmax(scores, axis=-1)
        out = attn @ v
        out = out @ o_proj
        return out + residual

    def _L0_attn_b_ref(x, D_param, log_dt, A_real_log, A_imag, C_re, C_im):
        import jax, jax.numpy as jnp
        import numpy as np
        T, B, H, N2 = (512, 2, 256, 8)

        def _s4d_kernel(log_dt, A_real_log, A_imag, C_re, C_im, L):
            dt = jnp.exp(log_dt)[:, None]
            A = -jnp.exp(A_real_log) + 1j * A_imag
            dtA = A * dt
            C = (C_re + 1j * C_im) * (jnp.exp(dtA) - 1.0) / A
            vander = jnp.exp(dtA[:, :, None] * jnp.arange(L))
            return 2.0 * jnp.einsum('hn,hnl->hl', C, vander).real
        seq_len = x.shape[0]
        residual = x * D_param
        xb = jnp.transpose(x, (1, 2, 0))
        k = _s4d_kernel(log_dt, A_real_log, A_imag, C_re, C_im, seq_len)
        n = 2 * seq_len
        k_f = jnp.fft.rfft(k, n=n)
        x_f = jnp.fft.rfft(xb, n=n)
        out = jnp.fft.irfft(x_f * k_f, n=n)[..., :seq_len]
        return jnp.transpose(out, (2, 0, 1)) + residual

    def _L0_ffn_ref(x, gate_w, up_w, down_w, gate_scale, up_scale, down_scale):
        import jax, jax.numpy as jnp
        import numpy as np
        B, S, H, I = (1, 64, 256, 768)

        def _quantized_matmul(x, w, scale):
            wq = w.astype(jnp.float8_e4m3fn).astype(x.dtype)
            y = jnp.einsum('bsi,io->bso', x, wq)
            return y * scale
        gate = jax.nn.silu(_quantized_matmul(x, gate_w, gate_scale))
        up = _quantized_matmul(x, up_w, up_scale)
        fuse = gate * up
        return _quantized_matmul(fuse, down_w, down_scale)
    x = L0_attn_a_x
    x = x + _L0_attn_a_ref(_layernorm(x, axis=-1), L0_attn_a_qkv, L0_attn_a_o_proj, L0_attn_a_gamma, L0_attn_a_beta)
    x = x + _L0_ffn_ref(_layernorm(x, axis=-1), L0_ffn_gate_w, L0_ffn_up_w, L0_ffn_down_w, L0_ffn_gate_scale, L0_ffn_up_scale, L0_ffn_down_scale)
    x = x + _L0_attn_b_ref(_layernorm(x, axis=-1), L0_attn_b_D_param, L0_attn_b_log_dt, L0_attn_b_A_real_log, L0_attn_b_A_imag, L0_attn_b_C_re, L0_attn_b_C_im)
    x = x + _L0_ffn_ref(_layernorm(x, axis=-1), L0_ffn_gate_w, L0_ffn_up_w, L0_ffn_down_w, L0_ffn_gate_scale, L0_ffn_up_scale, L0_ffn_down_scale)
    return x

_drawn_inputs = setup_inputs


def setup_inputs(seed=0):
    import zlib

    import numpy as np

    out = dict(_drawn_inputs(seed))
    spreads = {'L0_attn_a_gamma': (1.0, 0.6),
     'L0_attn_a_beta': (0.0, 0.529),
     'L0_attn_b_A_real_log': (-0.6931471824645996, 0.6)}
    factors = {'L0_ffn_gate_scale': 6.029,
     'L0_ffn_up_scale': 6.994,
     'L0_ffn_down_scale': 6.831,
     'L0_attn_b_log_dt': 29.568,
     'L0_attn_b_A_imag': 46.624,
     'L0_attn_b_C_re': 26.36,
     'L0_attn_b_C_im': 44.736}
    for name, (base, spread) in spreads.items():
        noise = np.random.default_rng([zlib.crc32(name.encode()), seed]).standard_normal(out[name].shape)
        drawn = base * np.exp(spread * noise) if base else spread * noise
        out[name] = jnp.asarray(drawn.astype(out[name].dtype))
    for name, factor in factors.items():
        out[name] = (out[name] * factor).astype(out[name].dtype)
    return out
```

```python
from contextlib import ExitStack

import numpy as np

import concourse.bass as bass
from concourse import mybir

F32 = mybir.dt.float32
F16 = mybir.dt.float16
BF16 = mybir.dt.bfloat16
U32 = mybir.dt.uint32
I32 = mybir.dt.int32
ALU = mybir.AluOpType
ACT = mybir.ActivationFunctionType
AX_X = mybir.AxisListType.X

P = 128
EPS = 1e-5
MASKED = -3.0e38
ROUND = 1.5 * 2.0**23
FP8_LARGEST = 464.0
LOG2E = float(np.float32(np.log2(np.e)))
LN2_HI = 0.693145751953125
LN2_LO = float(np.log(2.0) - LN2_HI)
TWO_PI = [6.28125, 0.0019340515136718750, float(2 * np.pi - 6.28125 - 0.0019340515136718750)]
PI_BELOW = float(np.nextafter(np.float32(np.pi), np.float32(0)))


def hybrid_layer(nc, x, qkv, o_proj, gamma, beta, d_param, log_dt, a_real_log, a_imag, c_re, c_im,
                 gate_w, up_w, down_w, gate_scale, up_scale, down_scale, out):
    B, S, H = x.shape
    KEY = qkv.shape[1] // 3
    I = gate_w.shape[1]
    N = a_imag.shape[1]
    T = S // P
    C = H // P
    M = I // P
    K = B * T
    HN = C * N
    assert KEY == H and C == 2 and T == 4 and B == 2 and H * 2 == 512

    ctx = ExitStack()
    with ctx:
        def sb(name, shape, dt=F32):
            return ctx.enter_context(nc.sbuf_tensor(name, shape, dt))

        def sem(name):
            return ctx.enter_context(nc.semaphore(name))

        x_in = sb("x_in", [P, K, H])
        x_plus = sb("x_plus", [P, K, H])
        x1 = sb("x1", [P, K, H])
        x2 = sb("x2", [P, K, H])
        x3 = x_plus
        x4 = x_in
        normed = sb("normed", [P, K, H])
        scaled_down = sb("scaled_down", [P, K, H])
        qkv_sb = sb("qkv_sb", [P, C, 3 * KEY])
        wo_sb = sb("wo_sb", [P, C, H])
        w_turned = sb("w_turned", [P, 3, C, H])
        wqk = sb("wqk", [P, C, H])
        wvo = sb("wvo", [P, C, H])
        xn_cols = sb("xn_cols", [P, B, C, S])
        g_cols = sb("g_cols", [P, B, C, S])
        v_rows = sb("v_rows", [P, B, T, H])
        probs = sb("probs", [P, 2, S])
        probs_cols = sb("probs_cols", [P, 2, S])
        neg_max = sb("neg_max", [P, K])
        row_sum = sb("row_sum", [P, K])
        inv_sum = sb("inv_sum", [P, K])
        gate_raw = sb("gate_raw", [P, C, I])
        up_raw = sb("up_raw", [P, C, I])
        down_raw = sb("down_raw", [P, M, H])
        grid = [sb(f"grid{w}", [P, C * I]) for w in range(3)]
        square = [sb(f"square{w}", [P, C * I], BF16) for w in range(3)]
        gate16 = sb("gate16", [P, C, I], F16)
        up16 = sb("up16", [P, C, I], F16)
        down_q = down_raw
        down16 = sb("down16", [P, M, H], BF16)
        max_square = sb("max_square", [P, 4])
        beyond = sb("beyond", [P, 4])
        down_scale_all = sb("down_scale_all", [P, H])
        ident = sb("ident", [P, P])
        ident16 = sb("ident16", [P, P], BF16)
        ones = sb("ones", [P, P])
        ones16 = sb("ones16", [P, 2], BF16)
        mask = sb("mask", [P, P], BF16)
        neg_half = sb("neg_half", [P, 2 * T])
        pos_half = sb("pos_half", [P, M])
        NR = 2 * M + 4 * C
        param_rows = sb("param_rows", [NR, P])
        params = sb("params", [P, NR])
        gate_scales, up_scales = params[:, 0:M], params[:, M:2 * M]
        gammas, betas = params[:, 2 * M:2 * M + C], params[:, 2 * M + C:2 * M + 2 * C]
        log_dts, d_params = params[:, 2 * M + 2 * C:2 * M + 3 * C], params[:, 2 * M + 3 * C:NR]
        stats = sb("stats", [P, 4, K, 6])
        mean_var = sb("mean_var", [P, 4, K, 2])
        var_eps = sb("var_eps", [P, 4, B, 2 * T])
        rstd = sb("rstd", [P, 4, B, 2 * T])
        one_rstd = sb("one_rstd", [P, B, T])
        mean_rstd = sb("mean_rstd", [P, 2, B, T])
        neg_mean_rstd = sb("neg_mean_rstd", [P, 2, B, T])
        bound = sb("bound", [P, 8, M])
        up_scales_fit = sb("up_scales_fit", [P, M])
        h_head = sb("h_head", [P, B, C, S], F16)
        h_tail = sb("h_tail", [P, B, C, S], F16)
        gated = sb("gated", [P, 2, S])
        fused = sb("fused", [P, 2, S])
        f_head = sb("f_head", [P, M, S], F16)
        f_tail = sb("f_tail", [P, M, S], F16)
        s4d_in = sb("s4d_in", [P, 4, HN])
        e_in = sb("e_in", [P, HN + C])
        s4d = sb("s4d", [P, 40, HN + C])
        two_k = sb("two_k", [P, HN + C], I32)
        taps = sb("taps", [P, 2, C])
        taps_all = sb("taps_all", [P, 2, H])
        x_lag = sb("x_lag", [P, T, H])
        x2_lag = sb("x2_lag", [P, T, H])
        psum = ctx.enter_context(nc.psum_tensor("psum", [P, 8, 512], F32))
        taps_dram = nc.dram_tensor("taps_dram", (2, H), F32)

        x_loaded = [sem(f"x_loaded{n}") for n in range(K // 2)]
        qkv_loaded, wo_loaded, rows_loaded, s4d_loaded = sem("qkv_loaded"), sem("wo_loaded"), sem("rows_loaded"), sem("s4d_loaded")
        w_loaded = [sem("gate_loaded"), sem("up_loaded"), sem("down_loaded")]
        down_scale_loaded = sem("down_scale_loaded")
        taps_stored, taps_loaded, out_stored = sem("taps_stored"), sem("taps_loaded"), sem("out_stored")
        pool_step = sem("pool_step")
        consts_ready = sem("consts_ready")
        params_turned, params_ready = sem("params_turned"), sem("params_ready")
        dve_step = sem("dve_step")
        stats_ready = [sem(f"stats_ready{n}") for n in range(4)]
        rstd_ready = [sem(f"rstd_ready{n}") for n in range(4)]
        z_ready, z_turned = sem("z_ready"), sem("z_turned")
        xn_by_act, xn_by_dve = sem("xn_by_act"), sem("xn_by_dve")
        w_turned_pe, wt_by_act, wt_by_dve = sem("w_turned_pe"), sem("wt_by_act"), sem("wt_by_dve")
        wqk_made, wvo_made, wqk_ready, wvo_ready = sem("wqk_made"), sem("wvo_made"), sem("wqk_ready"), sem("wvo_ready")
        g_made, g_by_act, g_by_dve = sem("g_made"), sem("g_by_act"), sem("g_by_dve")
        v_made, v_by_act, v_by_dve = sem("v_made"), sem("v_by_act"), sem("v_by_dve")
        x_plus_ready = sem("x_plus_ready")
        scores_made, max_ready, probs_ready = sem("scores_made"), sem("max_ready"), sem("probs_ready")
        probs_turned, probs_cols_ready = sem("probs_turned"), sem("probs_cols_ready")
        attn_made, x1_ready = sem("attn_made"), sem("x1_ready")
        squares_ready, norms_made, norms_read = sem("squares_ready"), sem("norms_made"), sem("norms_read")
        fit_ready, bound_squared, bound_ready = sem("fit_ready"), sem("bound_squared"), sem("bound_ready")
        grid_ready, gate_up_ready, down_ready = sem("grid_ready"), sem("gate_up_ready"), sem("down_ready")
        h_ready, h_turned, h_head_ready, h_tail_ready = sem("h_ready"), sem("h_turned"), sem("h_head_ready"), sem("h_tail_ready")
        gate_made, up_made, gated_ready = sem("gate_made"), sem("up_made"), sem("gated_ready")
        fused_ready, f_head_ready, f_tail_ready = sem("fused_ready"), sem("f_head_ready"), sem("f_tail_ready")
        down_made, down_read = sem("down_made"), sem("down_read")
        x2_ready, x3_ready, lag_ready, x4_ready = sem("x2_ready"), sem("x3_ready"), sem("lag_ready"), sem("x4_ready")
        tanh_in, tanh_out, trig_in, trig_out, taps_ready = sem("tanh_in"), sem("tanh_out"), sem("trig_in"), sem("trig_out"), sem("taps_ready")

        BANK_WT, BANK_WQK, BANK_WVO, BANK_PARAMS, BANK_NORMS = [4, 5, 6], 2, 3, 7, 5
        BANK_Z = [[0, 1], [4, 5]]
        BANK_G = [[6, 7], [0, 1]]
        BANK_V = [[2, 3], [4, 5]]
        BANK_S, BANK_PT, BANK_O = [6, 7], [2, 3], [0, 1]
        BANK_H, BANK_GATE, BANK_UP, BANK_DOWN = [4, 5], [6, 2], [7, 3], [0, 1]

        x_tiles = x.rearrange("b (t p) h -> p (b t) h", p=P)
        out_tiles = out.rearrange("b (t p) h -> p (b t) h", p=P)
        tile_of = [(b, t) for b in range(B) for t in range(T)]

        block = ctx.enter_context(nc.Block())

        @block.sync
        def _(sp):
            for n in range(2):
                sp.dma_start(x_in[:, 2 * n:2 * n + 2, :], x_tiles[:, 2 * n:2 * n + 2, :]).then_inc(x_loaded[n], 16)
            sp.dma_start(qkv_sb[:], qkv.rearrange("(c p) n -> p c n", p=P)).then_inc(qkv_loaded, 16)
            for n in range(2, 4):
                sp.dma_start(x_in[:, 2 * n:2 * n + 2, :], x_tiles[:, 2 * n:2 * n + 2, :]).then_inc(x_loaded[n], 16)
            sp.dma_start(wo_sb[:], o_proj.rearrange("(c p) n -> p c n", p=P)).then_inc(wo_loaded, 16)
            sp.dma_start(gate_raw[:], gate_w.rearrange("(c p) n -> p c n", p=P)).then_inc(w_loaded[0], 16)
            sp.dma_start(up_raw[:], up_w.rearrange("(c p) n -> p c n", p=P)).then_inc(w_loaded[1], 16)
            sp.dma_start(down_raw[:], down_w.rearrange("(c p) n -> p c n", p=P)).then_inc(w_loaded[2], 16)
            sp.dma_start(down_scale_all[:], down_scale.partition_broadcast(P)).then_inc(down_scale_loaded, 16)
            sp.wait_ge(taps_ready, 1)
            with nc.allow_non_contiguous_dma(reason="256 taps, one per partition"):
                for k in range(2):
                    sp.dma_start(taps_dram.ap()[k].rearrange("(c p) -> p c", p=P), taps[:, k, :]).then_inc(taps_stored, 16)
            sp.wait_ge(taps_stored, 32)
            sp.dma_start(taps_all[:], taps_dram.ap().partition_broadcast(P)).then_inc(taps_loaded, 16)
            for n in range(K // 2):
                sp.wait_ge(x4_ready, 2 * n + 2)
                sp.dma_start(out_tiles[:, 2 * n:2 * n + 2, :], x4[:, 2 * n:2 * n + 2, :]).then_inc(out_stored, 16)
            sp.wait_ge(out_stored, 16 * (K // 2))

        @block.gpsimd
        def _(pool):
            count = [0]

            def step(ins):
                count[0] += 1
                ins.then_inc(pool_step, 1)
                pool.wait_ge(pool_step, count[0])

            step(pool.memset(ident[:], 0.0))
            step(pool.affine_select(out=ident[:], in_=ident[:], compare_op=ALU.not_equal, fill=1.0, base=0,
                                    pattern=[[-1, P]], channel_multiplier=1))
            pool.memset(neg_half[:], -0.5)
            pool.memset(pos_half[:], 0.5)
            pool.memset(ones16[:], 1.0)
            pool.memset(ones[:], 1.0)
            step(pool.memset(mask[:], 0.0))
            pool.affine_select(out=mask[:], in_=mask[:], compare_op=ALU.is_ge, fill=MASKED, base=0,
                               pattern=[[-1, P]], channel_multiplier=1)
            pool.tensor_copy(ident16[:], ident[:]).then_inc(consts_ready, 1)

            def inverse_std(n, b, twice=False):
                pool.wait_ge(stats_ready[n], T * (b + 1))
                var = mean_var[:, n, T * b:T * b + T, 1]
                w = 2 * T if twice else T
                if twice:
                    pool.tensor_scalar(var_eps[:, n, b, T:w], var, 1.0 + EPS, EPS * EPS, ALU.mult, ALU.add)
                step(pool.tensor_scalar(var_eps[:, n, b, 0:T], var, EPS, 1.0, ALU.add, ALU.mult))
                pool.tensor_tensor(rstd[:, n, b, 0:w], var_eps[:, n, b, 0:w], neg_half[:, 0:w],
                                   ALU.pow).then_inc(rstd_ready[n], 1)
                pool.wait_ge(rstd_ready[n], b + 1)

            def shift_of(n, b):
                i = 0 if n == 0 else 1
                step(pool.tensor_tensor(mean_rstd[:, i, b, :], mean_var[:, n, T * b:T * b + T, 0],
                                        rstd[:, n, b, 0:T], ALU.mult))
                step(pool.tensor_scalar(neg_mean_rstd[:, i, b, :], mean_rstd[:, i, b, :], -1.0, 1.0, ALU.mult, ALU.mult))

            for b in range(B):
                inverse_std(0, b, twice=True)
            for b in range(B):
                shift_of(0, b)
                step(pool.tensor_scalar(one_rstd[:, b, :], rstd[:, 0, b, 0:T], 1.0, 1.0, ALU.add, ALU.mult))
                for t in range(T):
                    pool.tensor_scalar(x_plus[:, T * b + t, :], x_in[:, T * b + t, :], one_rstd[:, b, t:t + 1],
                                       neg_mean_rstd[:, 0, b, t:t + 1], ALU.mult, ALU.add).then_inc(x_plus_ready, 1)

            def to_grid(w, raw, rounded):
                pool.wait_ge(grid_ready, w + 1)
                flat = raw[:].rearrange("p c n -> p (c n)")
                step(pool.tensor_tensor(flat, flat, grid[w][:], ALU.add))
                return pool.tensor_tensor(rounded[:].rearrange("p c n -> p (c n)"), flat, grid[w][:], ALU.subtract)

            to_grid(0, gate_raw, gate16).then_inc(gate_up_ready, 1)
            pool.wait_ge(bound_squared, 1)
            pool.tensor_tensor(bound[:, 4, :], bound[:, 3, :], pos_half[:], ALU.pow).then_inc(bound_ready, 1)
            to_grid(1, up_raw, up16).then_inc(gate_up_ready, 1)
            inverse_std(1, 0)
            step(to_grid(2, down_raw, down_q))
            pool.wait_ge(fit_ready, 1)
            for m in range(M):
                pool.tensor_scalar(down16[:, m, :], down_q[:, m, :], bound[:, 6, m:m + 1], 1.0, ALU.mult,
                                   ALU.mult).then_inc(down_ready, 1)
            inverse_std(1, 1)

            def residual(n, new, old, b, ready):
                for t in range(T):
                    k = T * b + t
                    pool.wait_ge(down_read, K * n + k + 1)
                    pool.tensor_tensor(new[:, k, :], scaled_down[:, k, :], old[:, k, :], ALU.add).then_inc(ready, 1)

            residual(0, x2, x1, 0, x2_ready)
            inverse_std(2, 0)
            shift_of(2, 0)
            pool.wait_ge(taps_loaded, 16)
            for t in range(T):
                step(pool.tensor_scalar(x_lag[:, t, :], x2[:, t, :], rstd[:, 2, 0, t:t + 1],
                                        neg_mean_rstd[:, 1, 0, t:t + 1], ALU.mult, ALU.add))
                step(pool.tensor_tensor(x_lag[:, t, :], x_lag[:, t, :], taps_all[:, 1, :], ALU.mult))
            inverse_std(3, 0)
            residual(0, x2, x1, 1, x2_ready)
            inverse_std(2, 1)
            for t in range(T):
                pool.tensor_tensor(x2_lag[:, t, :], x2[:, T + t, :], x_lag[:, t, :], ALU.add).then_inc(lag_ready, 1)
            inverse_std(3, 1)
            for b in range(B):
                residual(1, x4, x3, b, x4_ready)

        @block.scalar
        def _(act):
            def chunks(vector):
                return vector.rearrange("(m p) -> m p", p=P)

            at = 0
            for vector in (gate_scale, up_scale, gamma, beta, log_dt, d_param):
                n = vector.shape[0] // P
                act.dma_start(param_rows[at:at + n, :], chunks(vector)).then_inc(rows_loaded, 16)
                at += n
            for n, array in enumerate((a_real_log, a_imag, c_re, c_im)):
                act.dma_start(s4d_in[:, n, :].rearrange("p (c n) -> p c n", c=C),
                              array.rearrange("(c p) n -> p c n", p=P)).then_inc(s4d_loaded, 16)

            for w in (0, 2):
                act.wait_ge(w_turned_pe, w + 1)
                act.activation(w_turned[:, w, :, :].rearrange("p c n -> p (c n)"), psum[:, BANK_WT[w], :],
                               ACT.Copy).then_inc(wt_by_act, 1)
            act.wait_ge(wqk_made, 1)
            act.activation(wqk[:].rearrange("p c n -> p (c n)"), psum[:, BANK_WQK, :], ACT.Copy).then_inc(wqk_ready, 1)

            def xn_chunk(b):
                act.wait_ge(params_ready, 1)
                act.wait_ge(z_turned, C * b + 1)
                act.activation(xn_cols[:, b, 0, :], psum[:, BANK_Z[b][0], :], ACT.Identity, scale=gammas[:, 0:1],
                               bias=betas[:, 0:1]).then_inc(xn_by_act, 1)

            def g_and_v(b):
                act.wait_ge(g_made, C * b + 1)
                act.activation(g_cols[:, b, 0, :], psum[:, BANK_G[b][0], :], ACT.Copy,
                               scale=float(KEY) ** -0.5).then_inc(g_by_act, 1)
                act.wait_ge(v_made, 2 * b + 1)
                act.activation(v_rows[:, b, 0:2, :].rearrange("p t n -> p (t n)"), psum[:, BANK_V[b][0], :],
                               ACT.Copy).then_inc(v_by_act, 1)

            xn_chunk(0)
            xn_chunk(1)
            g_and_v(0)
            act.wait_ge(tanh_in, 1)
            act.activation(s4d[:, 3, :], s4d[:, 2, :], ACT.Tanh, scale=0.5).then_inc(tanh_out, 1)
            g_and_v(1)
            for k in range(K + 1):
                if k < K:
                    W = P * (k % T + 1)
                    act.wait_ge(max_ready, k + 1)
                    if k >= 2:
                        act.wait_ge(probs_turned, k - 1)
                    act.activation(probs[:, k % 2, 0:W], psum[:, BANK_S[k % 2], 0:W], ACT.Exp,
                                   bias=neg_max[:, k:k + 1], accum_out=row_sum[:, k:k + 1]).then_inc(probs_ready, 1)
                if k >= 1:
                    j = k - 1
                    W = P * (j % T + 1)
                    act.wait_ge(probs_turned, k)
                    if j >= 2:
                        act.wait_ge(attn_made, j - 1)
                    act.activation(probs_cols[:, j % 2, 0:W], psum[:, BANK_PT[j % 2], 0:W],
                                   ACT.Copy).then_inc(probs_cols_ready, 1)
            act.wait_ge(trig_in, 1)
            act.activation(s4d[:, 10, 0:HN], s4d[:, 8, 0:HN], ACT.Tanh, scale=0.5)
            act.activation(s4d[:, 11, 0:HN], s4d[:, 9, 0:HN], ACT.Sin)
            act.activation(s4d[:, 12, 0:HN], s4d[:, 9, 0:HN], ACT.Sin, scale=0.5).then_inc(trig_out, 1)

            with act.Fori(0, 2) as f:
                for b in range(B):
                    n = f * B + b
                    for c in range(C):
                        act.wait_ge(h_turned, n * C + (c + 1))
                        act.activation(h_head[:, b, c, :], psum[:, BANK_H[c], :], ACT.Copy).then_inc(h_head_ready, 1)
                    for m in range(M):
                        act.wait_ge(gate_made, n * M + (m + 1))
                        act.activation(gated[:, m % 2, :], psum[:, BANK_GATE[m % 2], :], ACT.Silu,
                                       scale=gate_scales[:, m:m + 1]).then_inc(gated_ready, 1)
                        act.wait_ge(fused_ready, n * M + (m + 1))
                        act.activation(f_head[:, m, :], fused[:, m % 2, :], ACT.Copy).then_inc(f_head_ready, 1)

        @block.vector
        def _(dve):
            count = [0]

            def step(ins):
                count[0] += 1
                ins.then_inc(dve_step, 1)
                dve.wait_ge(dve_step, count[0])

            def tile_stats(n, k, source):
                step(dve.bn_stats(stats[:, n, k, :], source[:, k, :]))
                dve.bn_aggr(mean_var[:, n, k, :], stats[:, n, k, :]).then_inc(stats_ready[n], 1)

            def normalise(n, b, scale_at, ready):
                dve.wait_ge(rstd_ready[n], b + 1)
                for t in range(T):
                    k = T * b + t
                    src = (x_in, x1, None, x3)[n]
                    dve.tensor_scalar(normed[:, k, :], src[:, k, :], mean_var[:, n, k, 0:1],
                                      rstd[:, n, b, scale_at + t:scale_at + t + 1], ALU.subtract,
                                      ALU.mult).then_inc(ready, 1)

            for k in range(T):
                if k % 2 == 0:
                    dve.wait_ge(x_loaded[k // 2], 16)
                tile_stats(0, k, x_in)
            dve.wait_ge(params_turned, 1)
            dve.tensor_copy(params[:], psum[:, BANK_PARAMS, 0:NR]).then_inc(params_ready, 1)
            normalise(0, 0, T, z_ready)
            dve.wait_ge(w_turned_pe, 2)
            dve.tensor_copy(w_turned[:, 1, :, :].rearrange("p c n -> p (c n)"), psum[:, BANK_WT[1], :]).then_inc(wt_by_dve, 1)
            for k in range(T, K):
                if k % 2 == 0:
                    dve.wait_ge(x_loaded[k // 2], 16)
                tile_stats(0, k, x_in)

            def xn_chunk(b):
                dve.wait_ge(params_ready, 1)
                dve.wait_ge(z_turned, C * b + 2)
                dve.tensor_scalar(xn_cols[:, b, 1, :], psum[:, BANK_Z[b][1], :], gammas[:, 1:2], betas[:, 1:2],
                                  ALU.mult, ALU.add).then_inc(xn_by_dve, 1)

            def g_chunk(b):
                dve.wait_ge(g_made, C * b + 2)
                dve.tensor_scalar(g_cols[:, b, 1, :], psum[:, BANK_G[b][1], :], float(KEY) ** -0.5, None,
                                  ALU.mult).then_inc(g_by_dve, 1)

            def v_half(b):
                dve.wait_ge(v_made, 2 * b + 2)
                dve.tensor_copy(v_rows[:, b, 2:4, :].rearrange("p t n -> p (t n)"),
                                psum[:, BANK_V[b][1], :]).then_inc(v_by_dve, 1)

            W2 = HN + C
            st = lambda n, w=HN: s4d[:, n, 0:w]

            def exp_reduce():
                dve.wait_ge(s4d_loaded, 64)
                dve.tensor_copy(e_in[:, 0:HN], s4d_in[:, 0, :])
                step(dve.tensor_copy(e_in[:, HN:W2], log_dts))
                step(dve.tensor_scalar(st(0, W2), e_in[:], LOG2E, ROUND, ALU.mult, ALU.add))
                step(dve.tensor_scalar(st(0, W2), st(0, W2), -ROUND, None, ALU.add))
                step(dve.scalar_tensor_tensor(out=st(1, W2), in0=st(0, W2), scalar=-LN2_HI, in1=e_in[:], op0=ALU.mult, op1=ALU.add))
                step(dve.scalar_tensor_tensor(out=st(2, W2), in0=st(0, W2), scalar=-LN2_LO, in1=st(1, W2), op0=ALU.mult, op1=ALU.add))
                step(dve.tensor_scalar(st(4, W2), st(0, W2), -127.0, 128.0, ALU.max, ALU.min))
                dve.tensor_scalar(two_k[:], st(4, W2), 127.0, 2.0**23, ALU.add, ALU.mult).then_inc(tanh_in, 1)

            def exp_finish():
                dve.wait_ge(tanh_in, 1)
                dve.wait_ge(tanh_out, 1)
                step(dve.tensor_scalar(st(4, W2), st(3, W2), -1.0, 1.0, ALU.mult, ALU.add))
                step(dve.reciprocal(st(5, W2), st(4, W2)))
                step(dve.scalar_tensor_tensor(out=st(6, W2), in0=st(3, W2), scalar=1.0, in1=st(5, W2), op0=ALU.add, op1=ALU.mult))
                step(dve.tensor_tensor(st(7, W2), st(6, W2), two_k[:].bitcast(F32), ALU.mult))
                for c in range(C):
                    dt = s4d[:, 7, HN + c:HN + c + 1]
                    cs = slice(N * c, N * c + N)
                    dve.tensor_scalar(s4d[:, 8, cs], s4d[:, 7, cs], dt, -1.0, ALU.mult, ALU.mult)
                    step(dve.tensor_scalar(s4d[:, 13, cs], s4d_in[:, 1, cs], dt, None, ALU.mult))
                step(dve.tensor_scalar(st(14), st(13), 1.0 / (2.0 * np.pi), ROUND, ALU.mult, ALU.add))
                step(dve.tensor_scalar(st(14), st(14), -ROUND, None, ALU.add))
                for part in TWO_PI:
                    step(dve.scalar_tensor_tensor(out=st(13), in0=st(14), scalar=-part, in1=st(13), op0=ALU.mult, op1=ALU.add))
                dve.tensor_scalar(st(9), st(13), -PI_BELOW, PI_BELOW, ALU.max, ALU.min).then_inc(trig_in, 1)

            def taps_finish():
                w, cr, ci = s4d_in[:, 1, :], s4d_in[:, 2, :], s4d_in[:, 3, :]
                a = st(7)
                dve.wait_ge(trig_out, 1)
                step(dve.tensor_scalar(st(15), st(10), -1.0, 1.0, ALU.mult, ALU.add))
                step(dve.reciprocal(st(16), st(15)))
                step(dve.scalar_tensor_tensor(out=st(17), in0=st(10), scalar=2.0, in1=st(16), op0=ALU.mult, op1=ALU.mult))
                step(dve.tensor_scalar(st(18), st(17), 1.0, None, ALU.add))
                step(dve.scalar_tensor_tensor(out=st(19), in0=st(12), scalar=-2.0, in1=st(12), op0=ALU.mult, op1=ALU.mult))
                step(dve.tensor_tensor(st(20), st(18), st(19), ALU.mult))
                step(dve.tensor_tensor(st(21), st(20), st(17), ALU.add))
                step(dve.tensor_tensor(st(22), st(18), st(11), ALU.mult))
                step(dve.tensor_tensor(st(23), cr, st(21), ALU.mult))
                step(dve.tensor_tensor(st(24), ci, st(22), ALU.mult))
                step(dve.tensor_tensor(st(25), st(23), st(24), ALU.subtract))
                step(dve.tensor_tensor(st(23), cr, st(22), ALU.mult))
                step(dve.tensor_tensor(st(24), ci, st(21), ALU.mult))
                step(dve.tensor_tensor(st(26), st(23), st(24), ALU.add))
                step(dve.tensor_tensor(st(27), a, a, ALU.mult))
                step(dve.tensor_tensor(st(28), w, w, ALU.mult))
                step(dve.tensor_tensor(st(27), st(27), st(28), ALU.add))
                step(dve.reciprocal(st(29), st(27)))
                step(dve.tensor_tensor(st(30), st(25), a, ALU.mult))
                step(dve.tensor_tensor(st(31), st(26), w, ALU.mult))
                step(dve.tensor_tensor(st(32), st(31), st(30), ALU.subtract))
                step(dve.tensor_tensor(st(33), st(32), st(29), ALU.mult))
                step(dve.tensor_tensor(st(30), st(25), w, ALU.mult))
                step(dve.tensor_tensor(st(31), st(26), a, ALU.mult))
                step(dve.scalar_tensor_tensor(out=st(32), in0=st(30), scalar=-1.0, in1=st(31), op0=ALU.mult, op1=ALU.subtract))
                step(dve.tensor_tensor(st(34), st(32), st(29), ALU.mult))
                step(dve.scalar_tensor_tensor(out=st(35), in0=st(21), scalar=1.0, in1=st(33), op0=ALU.add, op1=ALU.mult))
                step(dve.tensor_tensor(st(36), st(34), st(22), ALU.mult))
                step(dve.tensor_tensor(st(37), st(35), st(36), ALU.subtract))
                dve.tensor_reduce(s4d[:, 38, 0:C], st(33).rearrange("p (c n) -> p c n", c=C), AX_X, ALU.add)
                step(dve.tensor_reduce(s4d[:, 39, 0:C], st(37).rearrange("p (c n) -> p c n", c=C), AX_X, ALU.add))
                dve.scalar_tensor_tensor(out=taps[:, 0, :], in0=s4d[:, 38, 0:C], scalar=2.0, in1=d_params, op0=ALU.mult, op1=ALU.add)
                dve.tensor_scalar(taps[:, 1, :], s4d[:, 39, 0:C], 2.0, None, ALU.mult).then_inc(taps_ready, 1)

            raws = (gate_raw, up_raw, down_raw)

            def weight_grid(w):
                dve.wait_ge(w_loaded[w], 16)
                flat = raws[w][:].rearrange("p c n -> p (c n)")
                dve.tensor_tensor_reduce(square[w][:], flat, flat, 1.0, 0.0, ALU.mult, ALU.max, max_square[:, w:w + 1])
                step(dve.tensor_scalar(grid[w][:].bitcast(U32), flat.bitcast(U32), 0x7F800000, None, ALU.bitwise_and))
                dve.tensor_scalar(grid[w][:], grid[w][:], 2.0**-6, 1.5 * 2.0**20, ALU.max, ALU.mult).then_inc(grid_ready, 1)

            def mark_beyond():
                dve.wait_ge(grid_ready, 3)
                step(dve.tensor_reduce(max_square[:, 3:4], max_square[:, 0:3], AX_X, ALU.max))
                dve.tensor_scalar(beyond[:, 0:1], max_square[:, 3:4], FP8_LARGEST**2, None, ALU.is_gt).then_inc(squares_ready, 1)

            def bound_gate_up():
                dve.wait_ge(norms_made, 1)
                dve.tensor_scalar(bound[:, 0, :], psum[:, BANK_NORMS, 0:M], 2.26, 5e-4, ALU.mult, ALU.add)
                dve.tensor_scalar(bound[:, 1, :], psum[:, BANK_NORMS, M:2 * M], 2.26, 5e-4, ALU.mult, ALU.add)
                step(dve.tensor_scalar(beyond[:, 1:2], psum[:, BANK_NORMS, 2 * M:2 * M + 1], 0.0, 3e38, ALU.is_gt, ALU.mult))
                norms_read_at = dve.tensor_scalar(beyond[:, 2:3], beyond[:, 1:2], 3e38, None, ALU.mult)
                norms_read_at.then_inc(norms_read, 1)
                step(dve.tensor_tensor(bound[:, 2, :], gate_scales, up_scales, ALU.mult))
                step(dve.tensor_tensor(bound[:, 2, :], bound[:, 2, :], bound[:, 2, :], ALU.mult))
                step(dve.tensor_tensor(bound[:, 1, :], bound[:, 1, :], bound[:, 0, :], ALU.mult))
                dve.scalar_tensor_tensor(out=bound[:, 3, :], in0=bound[:, 1, :], scalar=65536.0, in1=bound[:, 2, :],
                                         op0=ALU.mult, op1=ALU.mult).then_inc(bound_squared, 1)
                dve.wait_ge(norms_read, 1)
                step(dve.tensor_tensor(beyond[:, 3:4], beyond[:, 2:3], beyond[:, 2:3], ALU.subtract))
                dve.wait_ge(down_scale_loaded, 16)
                dve.tensor_scalar(down_scale_all[:], down_scale_all[:], beyond[:, 3:4], None, ALU.add)

            def fit_powers():
                dve.wait_ge(bound_ready, 1)
                step(dve.tensor_scalar(bound[:, 5, :].bitcast(U32), bound[:, 4, :].bitcast(U32), 0x7F800000, None, ALU.bitwise_and))
                step(dve.tensor_scalar(bound[:, 6, :], bound[:, 5, :], 2.0**-80, 2.0**-14, ALU.max, ALU.mult))
                step(dve.reciprocal(bound[:, 7, :], bound[:, 6, :]))
                dve.tensor_tensor(up_scales_fit[:], up_scales, bound[:, 7, :], ALU.mult).then_inc(fit_ready, 1)

            def row_max(k):
                dve.wait_ge(scores_made, k + 1)
                dve.tensor_reduce(neg_max[:, k:k + 1], psum[:, BANK_S[k % 2], 0:P * (k % T + 1)], AX_X, ALU.max,
                                  negate=True).then_inc(max_ready, 1)

            def attention_out(k):
                dve.wait_ge(probs_ready, k + 1)
                step(dve.reciprocal(inv_sum[:, k:k + 1], row_sum[:, k:k + 1]))
                dve.wait_ge(attn_made, k + 1)
                dve.wait_ge(x_plus_ready, k + 1)
                dve.scalar_tensor_tensor(out=x1[:, k, :], in0=psum[:, BANK_O[k % 2], 0:H], scalar=inv_sum[:, k:k + 1],
                                         in1=x_plus[:, k, :], op0=ALU.mult, op1=ALU.add).then_inc(x1_ready, 1)
                dve.wait_ge(x1_ready, k + 1)
                tile_stats(1, k, x1)

            xn_chunk(0)
            dve.wait_ge(wvo_made, 1)
            dve.tensor_copy(wvo[:].rearrange("p c n -> p (c n)"), psum[:, BANK_WVO, :]).then_inc(wvo_ready, 1)
            normalise(0, 1, T, z_ready)
            exp_reduce()
            xn_chunk(1)
            g_chunk(0)
            v_half(0)
            weight_grid(0)
            g_chunk(1)
            v_half(1)
            exp_finish()
            weight_grid(1)
            weight_grid(2)
            mark_beyond()
            for k in range(K + 2):
                if k < K:
                    row_max(k)
                if k >= 2:
                    attention_out(k - 2)
                if k == 4:
                    bound_gate_up()
                if k == 5:
                    fit_powers()
                if k == 7:
                    normalise(1, 0, 0, h_ready)
            taps_finish()
            normalise(1, 1, 0, h_ready)

            def ffn_scale(n, k):
                b, t = tile_of[k]
                dve.wait_ge(down_made, 2 * (B * n + b) + t // 2 + 1)
                dve.tensor_tensor(scaled_down[:, k, :], psum[:, BANK_DOWN[t // 2], H * (t % 2):H * (t % 2) + H],
                                  down_scale_all[:], ALU.mult).then_inc(down_read, 1)

            def x2_stats(k):
                dve.wait_ge(x2_ready, k + 1)
                tile_stats(2, k, x2)

            def s4d_mix(k):
                b, t = tile_of[k]
                dve.wait_ge(rstd_ready[2], b + 1)
                dve.wait_ge(taps_loaded, 16)
                step(dve.scalar_tensor_tensor(out=normed[:, k, :], in0=x2[:, k, :], scalar=mean_var[:, 2, k, 0:1],
                                              in1=taps_all[:, 0, :], op0=ALU.subtract, op1=ALU.mult))
                if b:
                    dve.wait_ge(lag_ready, t + 1)
                dve.scalar_tensor_tensor(out=x3[:, k, :], in0=normed[:, k, :], scalar=rstd[:, 2, b, t:t + 1],
                                         in1=x2_lag[:, t, :] if b else x2[:, k, :], op0=ALU.mult,
                                         op1=ALU.add).then_inc(x3_ready, 1)
                dve.wait_ge(x3_ready, k + 1)
                tile_stats(3, k, x3)

            def scale_pass(n, b):
                for k in range(T * b, T * b + T):
                    ffn_scale(n, k)

            def between(n, b, m):
                tiles = range(T * b, T * b + T)
                if n == 0:
                    if m == 1:
                        for k in tiles:
                            x2_stats(k)
                    if m == 3:
                        for k in list(tiles)[:2]:
                            s4d_mix(k)
                    if m == 4:
                        for k in list(tiles)[2:]:
                            s4d_mix(k)
                    if m == 5:
                        normalise(3, b, 0, h_ready)

            for f in range(2):
                for b in range(B):
                    n = B * f + b
                    for c in range(C):
                        dve.wait_ge(h_head_ready, C * n + c + 1)
                        dve.tensor_tensor(h_tail[:, b, c, :], psum[:, BANK_H[c], :], h_head[:, b, c, :],
                                          ALU.subtract).then_inc(h_tail_ready, 1)
                    for m in range(M):
                        i = M * n + m
                        dve.wait_ge(gated_ready, i + 1)
                        dve.wait_ge(up_made, i + 1)
                        dve.scalar_tensor_tensor(out=fused[:, m % 2, :], in0=psum[:, BANK_UP[m % 2], :],
                                                 scalar=up_scales_fit[:, m:m + 1], in1=gated[:, m % 2, :],
                                                 op0=ALU.mult, op1=ALU.mult).then_inc(fused_ready, 1)
                        if n >= 1 and m == 0:
                            scale_pass((n - 1) // B, (n - 1) % B)
                        dve.wait_ge(f_head_ready, i + 1)
                        dve.tensor_tensor(f_tail[:, m, :], fused[:, m % 2, :], f_head[:, m, :],
                                          ALU.subtract).then_inc(f_tail_ready, 1)
                        if n >= 1:
                            between((n - 1) // B, (n - 1) % B, m)
            scale_pass(1, 1)

        @block.tensor
        def _(pe):
            def column(bank, start, width):
                return psum[:, bank, start:start + width]

            pe.wait_ge(rows_loaded, 96)
            pe.wait_ge(consts_ready, 1)
            pe.transpose(column(BANK_PARAMS, 0, NR), param_rows[:], ident[0:NR, 0:NR]).then_inc(params_turned, 1)
            pe.wait_ge(qkv_loaded, 16)
            for w in range(3):
                for kc in range(C):
                    for c in range(C):
                        last = pe.transpose(column(BANK_WT[w], kc * H + c * P, P),
                                            qkv_sb[:, c, w * KEY + kc * P:w * KEY + kc * P + P], ident[:])
                last.then_inc(w_turned_pe, 1)

            def fold(bank, left, right):
                for c in range(C):
                    for kc in range(C):
                        last = pe.matmul(column(bank, c * H, H), w_turned[:, left, kc, c * P:c * P + P], right(kc),
                                         start=(kc == 0), stop=(kc == C - 1))
                return last

            def turn_z(b):
                for c in range(C):
                    for t in range(T):
                        if c == 0:
                            pe.wait_ge(z_ready, T * b + t + 1)
                        last = pe.transpose(column(BANK_Z[b][c], t * P, P), normed[:, T * b + t, c * P:c * P + P], ident[:])
                    last.then_inc(z_turned, 1)

            def make_g(b):
                pe.wait_ge(xn_by_act, b + 1)
                pe.wait_ge(xn_by_dve, b + 1)
                for j in range(C):
                    for c in range(C):
                        last = pe.matmul(column(BANK_G[b][j], 0, S), wqk[:, c, j * P:j * P + P], xn_cols[:, b, c, :],
                                         start=(c == 0), stop=(c == C - 1))
                    last.then_inc(g_made, 1)

            def make_v(b):
                for t in range(T):
                    for c in range(C):
                        last = pe.matmul(column(BANK_V[b][t // 2], H * (t % 2), H), xn_cols[:, b, c, t * P:t * P + P],
                                         wvo[:, c, :], start=(c == 0), stop=(c == C - 1))
                    if t % 2:
                        last.then_inc(v_made, 1)

            pe.wait_ge(wt_by_act, 1)
            pe.wait_ge(wt_by_dve, 1)
            fold(BANK_WQK, 0, lambda kc: w_turned[:, 1, kc, :]).then_inc(wqk_made, 1)
            turn_z(0)
            pe.wait_ge(wt_by_act, 2)
            pe.wait_ge(wo_loaded, 16)
            fold(BANK_WVO, 2, lambda kc: wo_sb[:, kc, :]).then_inc(wvo_made, 1)
            turn_z(1)
            pe.wait_ge(wqk_ready, 1)
            pe.wait_ge(params_ready, 1)
            make_g(0)
            pe.wait_ge(wvo_ready, 1)
            make_v(0)
            make_g(1)
            make_v(1)

            def scores(k):
                b, i = tile_of[k]
                if k == 0:
                    pe.wait_ge(g_by_act, 1)
                    pe.wait_ge(g_by_dve, 1)
                if k == T:
                    pe.wait_ge(g_by_act, 2)
                    pe.wait_ge(g_by_dve, 2)
                if k >= 2:
                    pe.wait_ge(probs_ready, k - 1)
                W = P * (i + 1)
                for j in range(C):
                    pe.matmul(column(BANK_S[k % 2], 0, W), g_cols[:, b, j, i * P:i * P + P], xn_cols[:, b, j, 0:W],
                              start=(j == 0), stop=(j == C - 1))
                pe.matmul(column(BANK_S[k % 2], i * P, P), ident16[:], mask[:], start=False, stop=True,
                          skip_group_check=True).then_inc(scores_made, 1)

            def turn_probs(k):
                pe.wait_ge(probs_ready, k + 1)
                if k == 0:
                    pe.wait_ge(v_by_act, 1)
                    pe.wait_ge(v_by_dve, 1)
                if k >= 2:
                    pe.wait_ge(probs_cols_ready, k - 1)
                for t in range(k % T + 1):
                    last = pe.transpose(column(BANK_PT[k % 2], t * P, P), probs[:, k % 2, t * P:t * P + P], ident[:])
                last.then_inc(probs_turned, 1)

            def attend(k):
                b, i = tile_of[k]
                pe.wait_ge(probs_cols_ready, k + 1)
                if k == T:
                    pe.wait_ge(v_by_act, 2)
                    pe.wait_ge(v_by_dve, 2)
                if k >= 2:
                    pe.wait_ge(x1_ready, k - 1)
                for t in range(i + 1):
                    last = pe.matmul(column(BANK_O[k % 2], 0, H), probs_cols[:, k % 2, t * P:t * P + P],
                                     v_rows[:, b, t, :], start=(t == 0), stop=(t == i))
                last.then_inc(attn_made, 1)

            def channel_norms():
                pe.wait_ge(squares_ready, 1)
                pe.wait_ge(v_by_dve, 2)
                for w in range(2):
                    for m in range(M):
                        for c in range(C):
                            pe.matmul(column(BANK_NORMS, M * w + m, 1), square[w][:, c * I + m * P:c * I + m * P + P],
                                      ones16[:, 0:1], start=(c == 0), stop=(c == C - 1))
                pe.matmul(column(BANK_NORMS, 2 * M, 1), ones[:], beyond[:, 0:1], start=True,
                          stop=True).then_inc(norms_made, 1)

            for k in range(K + 2):
                if k < K:
                    scores(k)
                if 1 <= k <= K:
                    turn_probs(k - 1)
                if k == 3:
                    channel_norms()
                if k >= 2:
                    attend(k - 2)

            pe.wait_ge(norms_read, 1)
            pe.wait_ge(gate_up_ready, 2)
            with pe.Fori(0, 2) as f:
                def turn_h(b):
                    n = f * B + b
                    pe.wait_ge(h_ready, n * T + T)
                    if b:
                        pe.wait_ge(h_tail_ready, n * C)
                    for c in range(C):
                        for t in range(T):
                            last = pe.transpose(column(BANK_H[c], t * P, P), normed[:, T * b + t, c * P:c * P + P], ident[:])
                        last.then_inc(h_turned, 1)

                def gate_up(b, m):
                    n = f * B + b
                    for w, banks, made, read in ((gate16, BANK_GATE, gate_made, gated_ready), (up16, BANK_UP, up_made, fused_ready)):
                        if (b, m) >= (0, 2):
                            pe.wait_ge(read, n * M + m - 1)
                        for part, ready in ((h_head, h_head_ready), (h_tail, h_tail_ready)):
                            for c in range(C):
                                if m == 0 and w is gate16:
                                    pe.wait_ge(ready, n * C + (c + 1))
                                last = pe.matmul(column(banks[m % 2], 0, S), w[:, c, m * P:m * P + P], part[:, b, c, :],
                                                 start=(part is h_head and c == 0), stop=(part is h_tail and c == C - 1))
                        last.then_inc(made, 1)

                def down(b, m):
                    n = f * B + b
                    pe.wait_ge(f_tail_ready, n * M + (m + 1))
                    if b == 0:
                        pe.wait_ge(down_ready, m + 1)
                    for t in range(T):
                        for part in (f_head, f_tail):
                            last = pe.matmul(column(BANK_DOWN[t // 2], H * (t % 2), H), part[:, m, t * P:t * P + P],
                                             down16[:, m, :], start=(m == 0 and t % 2 == 0 and part is f_head),
                                             stop=(m == M - 1 and part is f_tail), skip_group_check=True)
                        if m == M - 1 and t % 2:
                            last.then_inc(down_made, 1)

                turn_h(0)
                for b in range(B):
                    for m in range(M):
                        gate_up(b, m)
                        if m >= 2:
                            down(b, m - 2)
                    if b + 1 < B:
                        turn_h(b + 1)
                    down(b, M - 2)
                    down(b, M - 1)


_INS = ['x', 'qkv', 'o_proj', 'gamma', 'beta', 'd_param', 'log_dt', 'a_real_log', 'a_imag', 'c_re', 'c_im',
        'gate_w', 'up_w', 'down_w', 'gate_scale', 'up_scale', 'down_scale']


def kernel(L0_attn_a_x, L0_attn_a_qkv, L0_attn_a_o_proj, L0_attn_a_gamma, L0_attn_a_beta, L0_attn_b_D_param,
           L0_attn_b_log_dt, L0_attn_b_A_real_log, L0_attn_b_A_imag, L0_attn_b_C_re, L0_attn_b_C_im, L0_ffn_gate_w,
           L0_ffn_up_w, L0_ffn_down_w, L0_ffn_gate_scale, L0_ffn_up_scale, L0_ffn_down_scale):
    import concourse.bacc as bacc
    from concourse.bass_utils import run_bass_kernel_spmd

    given = (L0_attn_a_x, L0_attn_a_qkv, L0_attn_a_o_proj, L0_attn_a_gamma, L0_attn_a_beta, L0_attn_b_D_param,
             L0_attn_b_log_dt, L0_attn_b_A_real_log, L0_attn_b_A_imag, L0_attn_b_C_re, L0_attn_b_C_im, L0_ffn_gate_w,
             L0_ffn_up_w, L0_ffn_down_w, L0_ffn_gate_scale, L0_ffn_up_scale, L0_ffn_down_scale)
    nc = bacc.Bacc("TRN2", target_bir_lowering=False, num_devices=1)
    arrays, aps = {}, []
    for name, value in zip(_INS, given):
        array = np.ascontiguousarray(value)
        arrays[f"in_{name}"] = array
        aps.append(nc.dram_tensor(f"in_{name}", array.shape, mybir.dt.from_np(array.dtype), kind="ExternalInput").ap())
    out = nc.dram_tensor("out", arrays["in_x"].shape, F32, kind="ExternalOutput").ap()
    hybrid_layer(nc, *aps, out)
    result = run_bass_kernel_spmd(nc, [arrays], core_ids=[0])
    return result.results[0]["out"]
```

```python
from contextlib import ExitStack

import numpy as np

import concourse.bass as bass
from concourse import mybir

F32 = mybir.dt.float32
F16 = mybir.dt.float16
BF16 = mybir.dt.bfloat16
U32 = mybir.dt.uint32
I32 = mybir.dt.int32
ALU = mybir.AluOpType
ACT = mybir.ActivationFunctionType
AX_X = mybir.AxisListType.X

P = 128
EPS = 1e-5
MASKED = -3.0e38
WARM_UP = 24
ROUND = 1.5 * 2.0**23
FP8_LARGEST = 464.0
LOG2E = float(np.float32(np.log2(np.e)))
LN2_HI = 0.693145751953125
LN2_LO = float(np.log(2.0) - LN2_HI)
TWO_PI = [6.28125, 0.0019340515136718750, float(2 * np.pi - 6.28125 - 0.0019340515136718750)]
PI_BELOW = float(np.nextafter(np.float32(np.pi), np.float32(0)))


def hybrid_layer(nc, x, qkv, o_proj, gamma, beta, d_param, log_dt, a_real_log, a_imag, c_re, c_im,
                 gate_w, up_w, down_w, gate_scale, up_scale, down_scale, out):
    B, S, H = x.shape
    KEY = qkv.shape[1] // 3
    I = gate_w.shape[1]
    N = a_imag.shape[1]
    T = S // P
    C = H // P
    M = I // P
    K = B * T
    HN = C * N
    assert KEY == H and C == 2 and T == 4 and B == 2 and H * 2 == 512

    ctx = ExitStack()
    with ctx:
        def sb(name, shape, dt=F32):
            return ctx.enter_context(nc.sbuf_tensor(name, shape, dt))

        def sem(name):
            return ctx.enter_context(nc.semaphore(name))

        x_in = sb("x_in", [P, K, H])
        x_plus = sb("x_plus", [P, K, H])
        x1 = sb("x1", [P, K, H])
        x2 = sb("x2", [P, K, H])
        x3 = x_plus
        x4 = x_in
        normed = sb("normed", [P, K, H])
        scaled_down = sb("scaled_down", [P, K, H])
        qkv_sb = sb("qkv_sb", [P, C, 3 * KEY])
        wo_sb = sb("wo_sb", [P, C, H])
        w_turned = sb("w_turned", [P, 3, C, H])
        wqk = sb("wqk", [P, C, H])
        wvo = sb("wvo", [P, C, H])
        xn_cols = sb("xn_cols", [P, B, C, S])
        g_cols = sb("g_cols", [P, B, C, S])
        v_rows = sb("v_rows", [P, B, T, H])
        probs = sb("probs", [P, 2, S])
        probs_cols = sb("probs_cols", [P, 2, S])
        neg_max = sb("neg_max", [P, K])
        row_sum = sb("row_sum", [P, K])
        inv_sum = sb("inv_sum", [P, K])
        gate_raw = sb("gate_raw", [P, C, I])
        up_raw = sb("up_raw", [P, C, I])
        down_raw = sb("down_raw", [P, M, H])
        grid = [sb(f"grid{w}", [P, C * I]) for w in range(3)]
        square = [sb(f"square{w}", [P, C * I], BF16) for w in range(3)]
        gate16 = sb("gate16", [P, C, I], F16)
        up16 = sb("up16", [P, C, I], F16)
        down_q = down_raw
        down16 = sb("down16", [P, M, H], BF16)
        max_square = sb("max_square", [P, 4])
        beyond = sb("beyond", [P, 4])
        down_scale_all = sb("down_scale_all", [P, H])
        ident = sb("ident", [P, P])
        ident16 = sb("ident16", [P, P], BF16)
        ones = sb("ones", [P, P])
        ones16 = sb("ones16", [P, 2], BF16)
        mask = sb("mask", [P, P], BF16)
        neg_half = sb("neg_half", [P, K])
        pos_half = sb("pos_half", [P, M])
        NR = 2 * M + 4 * C
        param_rows = sb("param_rows", [NR, P])
        params = sb("params", [P, NR])
        gate_scales, up_scales = params[:, 0:M], params[:, M:2 * M]
        gammas, betas = params[:, 2 * M:2 * M + C], params[:, 2 * M + C:2 * M + 2 * C]
        log_dts, d_params = params[:, 2 * M + 2 * C:2 * M + 3 * C], params[:, 2 * M + 3 * C:NR]
        stats = sb("stats", [P, 4, K, 6])
        mean_var = sb("mean_var", [P, 4, K, 2])
        var_eps = sb("var_eps", [P, 5, K])
        rstd = sb("rstd", [P, 5, K])
        one_rstd = sb("one_rstd", [P, K])
        mean_rstd = sb("mean_rstd", [P, 2, K])
        neg_mean_rstd = sb("neg_mean_rstd", [P, 2, K])
        bound = sb("bound", [P, 8, M])
        up_scales_fit = sb("up_scales_fit", [P, M])
        h_head = sb("h_head", [P, B, C, S], F16)
        h_tail = sb("h_tail", [P, B, C, S], F16)
        gated = sb("gated", [P, 2, S])
        FUSED = 3
        fused = sb("fused", [P, FUSED, S])
        f_head = sb("f_head", [P, M, S], F16)
        f_tail = sb("f_tail", [P, M, S], F16)
        s4d_in = sb("s4d_in", [P, 4, HN])
        e_in = sb("e_in", [P, HN + C])
        s4d = sb("s4d", [P, 40, HN + C])
        two_k = sb("two_k", [P, HN + C], I32)
        taps = sb("taps", [P, 2, C])
        taps_all = sb("taps_all", [P, 2, H])
        x_lag = sb("x_lag", [P, T, H])
        x2_lag = sb("x2_lag", [P, T, H])
        psum = ctx.enter_context(nc.psum_tensor("psum", [P, 8, 512], F32))
        taps_dram = nc.dram_tensor("taps_dram", (2, H), F32)

        x_loaded = [sem(f"x_loaded{n}") for n in range(K // 2)]
        qk_loaded, v_loaded, wo_loaded, rows_loaded, s4d_loaded = sem("qk_loaded"), sem("v_loaded"), sem("wo_loaded"), sem("rows_loaded"), sem("s4d_loaded")
        w_loaded = [sem("gate_loaded"), sem("up_loaded"), sem("down_loaded")]
        down_scale_loaded = sem("down_scale_loaded")
        taps_stored, taps_loaded, out_stored = sem("taps_stored"), sem("taps_loaded"), sem("out_stored")
        pool_step = sem("pool_step")
        ident_ready, consts_ready = sem("ident_ready"), sem("consts_ready")
        params_turned, params_ready = sem("params_turned"), sem("params_ready")
        dve_step = sem("dve_step")
        stats_ready = [sem(f"stats_ready{n}") for n in range(4)]
        rstd_ready = [sem(f"rstd_ready{n}") for n in range(4)]
        z_ready, z_turned = sem("z_ready"), sem("z_turned")
        xn_by_act, xn_by_dve = sem("xn_by_act"), sem("xn_by_dve")
        w_turned_pe, wt_by_act, wt_by_dve = sem("w_turned_pe"), sem("wt_by_act"), sem("wt_by_dve")
        wqk_made, wvo_made, wqk_ready, wvo_ready = sem("wqk_made"), sem("wvo_made"), sem("wqk_ready"), sem("wvo_ready")
        g_made, g_by_act, g_by_dve = sem("g_made"), sem("g_by_act"), sem("g_by_dve")
        v_made, v_by_act, v_by_dve = sem("v_made"), sem("v_by_act"), sem("v_by_dve")
        x_plus_ready = sem("x_plus_ready")
        scores_made, max_ready, probs_ready = sem("scores_made"), sem("max_ready"), sem("probs_ready")
        probs_turned, probs_cols_ready = sem("probs_turned"), sem("probs_cols_ready")
        attn_made, x1_ready = sem("attn_made"), sem("x1_ready")
        squares_ready, norms_made, norms_read = sem("squares_ready"), sem("norms_made"), sem("norms_read")
        fit_ready, bound_squared, bound_ready = sem("fit_ready"), sem("bound_squared"), sem("bound_ready")
        grid_ready, gate_up_ready, down_ready = sem("grid_ready"), sem("gate_up_ready"), sem("down_ready")
        h_ready, h_turned, h_head_ready, h_tail_ready = sem("h_ready"), sem("h_turned"), sem("h_head_ready"), sem("h_tail_ready")
        gate_made, up_made, gated_ready = sem("gate_made"), sem("up_made"), sem("gated_ready")
        fused_ready, f_head_ready = sem("fused_ready"), sem("f_head_ready")
        f_tail_by_pool, f_tail_by_dve = sem("f_tail_by_pool"), sem("f_tail_by_dve")
        down_made, down_read = sem("down_made"), sem("down_read")
        x2_ready, x3_ready, lag_ready, x4_ready = sem("x2_ready"), sem("x3_ready"), sem("lag_ready"), sem("x4_ready")
        tanh_in, tanh_out, trig_in, trig_out, taps_ready = sem("tanh_in"), sem("tanh_out"), sem("trig_in"), sem("trig_out"), sem("taps_ready")

        POOL_TAILS = (1, 3, 5)
        DVE_TAILS = tuple(m for m in range(M) if m not in POOL_TAILS)

        BANK_WT, BANK_WQK, BANK_WVO, BANK_PARAMS, BANK_NORMS = [4, 5, 3], 2, 3, 7, 5
        BANK_Z = [[0, 1], [4, 5]]
        BANK_G = [[6, 7], [0, 1]]
        BANK_V = [[2, 3], [4, 5]]
        BANK_S, BANK_PT, BANK_O = [6, 7], [2, 3], [0, 1]
        BANK_H, BANK_GATE, BANK_UP, BANK_DOWN = [4, 5], [6, 2], [7, 3], [0, 1]

        x_tiles = x.rearrange("b (t p) h -> p (b t) h", p=P)
        out_tiles = out.rearrange("b (t p) h -> p (b t) h", p=P)
        tile_of = [(b, t) for b in range(B) for t in range(T)]

        block = ctx.enter_context(nc.Block())

        @block.sync
        def _(sp):
            def load_x(n):
                sp.dma_start(x_in[:, 2 * n:2 * n + 2, :], x_tiles[:, 2 * n:2 * n + 2, :]).then_inc(x_loaded[n], 16)

            def load_chunks(to, array, loaded):
                sp.dma_start(to, array.rearrange("(c p) n -> p c n", p=P)).then_inc(loaded, 16)

            load_x(0)
            load_x(1)
            load_chunks(qkv_sb[:, :, 0:2 * KEY], qkv[:, 0:2 * KEY], qk_loaded)
            at = 0
            for vector in (gate_scale, up_scale, gamma, beta, log_dt, d_param):
                n = vector.shape[0] // P
                sp.dma_start(param_rows[at:at + n, :], vector.rearrange("(m p) -> m p", p=P)).then_inc(rows_loaded, 16)
                at += n
            load_x(2)
            load_x(3)
            load_chunks(qkv_sb[:, :, 2 * KEY:], qkv[:, 2 * KEY:], v_loaded)
            load_chunks(wo_sb[:], o_proj, wo_loaded)
            load_chunks(gate_raw[:], gate_w, w_loaded[0])
            load_chunks(up_raw[:], up_w, w_loaded[1])
            for n, array in enumerate((a_real_log, a_imag, c_re, c_im)):
                load_chunks(s4d_in[:, n, :].rearrange("p (c n) -> p c n", c=C), array, s4d_loaded)
            load_chunks(down_raw[:], down_w, w_loaded[2])
            sp.dma_start(down_scale_all[:], down_scale.partition_broadcast(P)).then_inc(down_scale_loaded, 16)
            sp.wait_ge(taps_ready, 1)
            with nc.allow_non_contiguous_dma(reason="256 taps, one per partition"):
                for k in range(2):
                    sp.dma_start(taps_dram.ap()[k].rearrange("(c p) -> p c", p=P), taps[:, k, :]).then_inc(taps_stored, 16)
            sp.wait_ge(taps_stored, 32)
            sp.dma_start(taps_all[:], taps_dram.ap().partition_broadcast(P)).then_inc(taps_loaded, 16)
            for n in range(K // 2):
                sp.wait_ge(x4_ready, 2 * n + 2)
                sp.dma_start(out_tiles[:, 2 * n:2 * n + 2, :], x4[:, 2 * n:2 * n + 2, :]).then_inc(out_stored, 16)
            sp.wait_ge(out_stored, 16 * (K // 2))

        @block.gpsimd
        def _(pool):
            count = [0]

            def step(ins):
                count[0] += 1
                ins.then_inc(pool_step, 1)
                pool.wait_ge(pool_step, count[0])

            step(pool.memset(ident[:], 0.0))
            pool.affine_select(out=ident[:], in_=ident[:], compare_op=ALU.not_equal, fill=1.0, base=0,
                               pattern=[[-1, P]], channel_multiplier=1).then_inc(ident_ready, 1)
            step(pool.memset(neg_half[:], -0.5))

            def inverse_std(n, k, count=1, twice=False):
                pool.wait_ge(stats_ready[n], k + count)
                factor, eps = (1.0 + EPS, EPS * EPS) if twice else (1.0, EPS)
                step(pool.tensor_scalar(var_eps[:, n, k:k + count], mean_var[:, n, k:k + count, 1], factor, eps, ALU.mult, ALU.add))
                pool.tensor_tensor(rstd[:, n, k:k + count], var_eps[:, n, k:k + count], neg_half[:, 0:count],
                                   ALU.pow).then_inc(rstd_ready[n], count)

            for k in range(K):
                inverse_std(0, k, twice=True)
                if k == T - 1:
                    pool.memset(pos_half[:], 0.5)
                    pool.memset(ones16[:], 1.0)
                    pool.memset(ones[:], 1.0)
                    step(pool.memset(mask[:], 0.0))
                    pool.affine_select(out=mask[:], in_=mask[:], compare_op=ALU.is_ge, fill=MASKED, base=0,
                                       pattern=[[-1, P]], channel_multiplier=1)
                    pool.tensor_copy(ident16[:], ident[:]).then_inc(consts_ready, 1)

            step(pool.tensor_scalar(var_eps[:, 4, :], mean_var[:, 0, :, 1], EPS, 1.0, ALU.add, ALU.mult))
            step(pool.tensor_tensor(rstd[:, 4, :], var_eps[:, 4, :], neg_half[:], ALU.pow))
            pool.tensor_scalar(one_rstd[:], rstd[:, 4, :], 1.0, 1.0, ALU.add, ALU.mult)
            step(pool.tensor_tensor(mean_rstd[:, 0, :], mean_var[:, 0, :, 0], rstd[:, 4, :], ALU.mult))
            step(pool.tensor_scalar(neg_mean_rstd[:, 0, :], mean_rstd[:, 0, :], -1.0, 1.0, ALU.mult, ALU.mult))
            for k in range(K):
                pool.tensor_scalar(x_plus[:, k, :], x_in[:, k, :], one_rstd[:, k:k + 1],
                                   neg_mean_rstd[:, 0, k:k + 1], ALU.mult, ALU.add).then_inc(x_plus_ready, 1)

            def to_grid(w, raw, rounded):
                pool.wait_ge(grid_ready, w + 1)
                flat = raw[:].rearrange("p c n -> p (c n)")
                step(pool.tensor_tensor(flat, flat, grid[w][:], ALU.add))
                return pool.tensor_tensor(rounded[:].rearrange("p c n -> p (c n)"), flat, grid[w][:], ALU.subtract)

            to_grid(0, gate_raw, gate16).then_inc(gate_up_ready, 1)
            to_grid(1, up_raw, up16).then_inc(gate_up_ready, 1)
            step(to_grid(2, down_raw, down_q))
            pool.wait_ge(bound_squared, 1)
            pool.tensor_tensor(bound[:, 4, :], bound[:, 3, :], pos_half[:], ALU.pow).then_inc(bound_ready, 1)
            inverse_std(1, 0, T)
            pool.wait_ge(fit_ready, 1)
            for m in range(M):
                pool.tensor_scalar(down16[:, m, :], down_q[:, m, :], bound[:, 6, m:m + 1], 1.0, ALU.mult,
                                   ALU.mult).then_inc(down_ready, 1)
            for k in range(T, K):
                inverse_std(1, k)

            def tail(n, m):
                pool.wait_ge(f_head_ready, M * n + m + 1)
                pool.tensor_tensor(f_tail[:, m, :], fused[:, m % FUSED, :], f_head[:, m, :],
                                   ALU.subtract).then_inc(f_tail_by_pool, 1)

            def residual(n, new, old, b, ready):
                for k in range(T * b, T * b + T):
                    pool.wait_ge(down_read, K * n + k + 1)
                    pool.tensor_tensor(new[:, k, :], scaled_down[:, k, :], old[:, k, :], ALU.add).then_inc(ready, 1)

            def lag_tap():
                step(pool.tensor_tensor(mean_rstd[:, 1, 0:T], mean_var[:, 2, 0:T, 0], rstd[:, 2, 0:T], ALU.mult))
                step(pool.tensor_scalar(neg_mean_rstd[:, 1, 0:T], mean_rstd[:, 1, 0:T], -1.0, 1.0, ALU.mult, ALU.mult))
                pool.wait_ge(taps_loaded, 16)
                for t in range(T):
                    step(pool.tensor_scalar(x_lag[:, t, :], x2[:, t, :], rstd[:, 2, t:t + 1],
                                            neg_mean_rstd[:, 1, t:t + 1], ALU.mult, ALU.add))
                    step(pool.tensor_tensor(x_lag[:, t, :], x_lag[:, t, :], taps_all[:, 1, :], ALU.mult))

            for n in range(2 * B):
                f, b = (n - 1) // B, (n - 1) % B
                for m in range(M):
                    if m == 1 and n in (1, 2):
                        residual(0, x2, x1, b, x2_ready)
                    if m == 1 and n == 3:
                        residual(1, x4, x3, b, x4_ready)
                    if m == 3 and n in (1, 2):
                        for k in range(T * b, T * b + T):
                            inverse_std(2, k)
                    if m == 5 and n in (1, 2):
                        if n == 2:
                            for t in range(T):
                                pool.tensor_tensor(x2_lag[:, t, :], x2[:, T + t, :], x_lag[:, t, :], ALU.add).then_inc(lag_ready, 1)
                        for k in range(T * b, T * b + T):
                            inverse_std(3, k)
                    if m in POOL_TAILS:
                        tail(n, m)
                if n == 1:
                    lag_tap()
            residual(1, x4, x3, 1, x4_ready)

        @block.scalar
        def _(act):
            def turned(w):
                act.wait_ge(w_turned_pe, w + 1)
                act.activation(w_turned[:, w, :, :].rearrange("p c n -> p (c n)"), psum[:, BANK_WT[w], :],
                               ACT.Copy).then_inc(wt_by_act, 1)

            def xn_chunk(b):
                act.wait_ge(params_ready, 1)
                act.wait_ge(z_turned, C * b + 1)
                act.activation(xn_cols[:, b, 0, :], psum[:, BANK_Z[b][0], :], ACT.Identity, scale=gammas[:, 0:1],
                               bias=betas[:, 0:1]).then_inc(xn_by_act, 1)

            def g_part(b):
                act.wait_ge(g_made, C * b + 1)
                act.activation(g_cols[:, b, 0, :], psum[:, BANK_G[b][0], :], ACT.Copy,
                               scale=float(KEY) ** -0.5).then_inc(g_by_act, 1)

            def v_part(b):
                act.wait_ge(v_made, 2 * b + 1)
                act.activation(v_rows[:, b, 0:2, :].rearrange("p t n -> p (t n)"), psum[:, BANK_V[b][0], :],
                               ACT.Copy).then_inc(v_by_act, 1)

            turned(0)
            xn_chunk(0)
            act.wait_ge(wqk_made, 1)
            act.activation(wqk[:].rearrange("p c n -> p (c n)"), psum[:, BANK_WQK, :], ACT.Copy).then_inc(wqk_ready, 1)
            turned(2)
            act.wait_ge(wvo_made, 1)
            act.activation(wvo[:].rearrange("p c n -> p (c n)"), psum[:, BANK_WVO, :], ACT.Copy).then_inc(wvo_ready, 1)
            xn_chunk(1)
            g_part(0)
            v_part(0)
            act.wait_ge(tanh_in, 1)
            act.activation(s4d[:, 3, :], s4d[:, 2, :], ACT.Tanh, scale=0.5).then_inc(tanh_out, 1)
            g_part(1)
            v_part(1)
            act.wait_ge(trig_in, 1)
            act.activation(s4d[:, 10, 0:HN], s4d[:, 8, 0:HN], ACT.Tanh, scale=0.5)
            act.activation(s4d[:, 11, 0:HN], s4d[:, 9, 0:HN], ACT.Sin)
            act.activation(s4d[:, 12, 0:HN], s4d[:, 9, 0:HN], ACT.Sin, scale=0.5).then_inc(trig_out, 1)
            for k in range(K + 1):
                if k < K:
                    W = P * (k % T + 1)
                    act.wait_ge(max_ready, k + 1)
                    if k >= 2:
                        act.wait_ge(probs_turned, k - 1)
                    act.activation(probs[:, k % 2, 0:W], psum[:, BANK_S[k % 2], 0:W], ACT.Exp,
                                   bias=neg_max[:, k:k + 1], accum_out=row_sum[:, k:k + 1]).then_inc(probs_ready, 1)
                if k >= 1:
                    j = k - 1
                    W = P * (j % T + 1)
                    act.wait_ge(probs_turned, k)
                    if j >= 2:
                        act.wait_ge(attn_made, j - 1)
                    act.activation(probs_cols[:, j % 2, 0:W], psum[:, BANK_PT[j % 2], 0:W],
                                   ACT.Copy).then_inc(probs_cols_ready, 1)
            with act.Fori(0, 2) as f:
                for b in range(B):
                    n = f * B + b
                    for c in range(C):
                        act.wait_ge(h_turned, n * C + (c + 1))
                        act.activation(h_head[:, b, c, :], psum[:, BANK_H[c], :], ACT.Copy).then_inc(h_head_ready, 1)
                    for m in range(M):
                        act.wait_ge(gate_made, n * M + (m + 1))
                        act.activation(gated[:, m % 2, :], psum[:, BANK_GATE[m % 2], :], ACT.Silu,
                                       scale=gate_scales[:, m:m + 1]).then_inc(gated_ready, 1)
                        act.wait_ge(fused_ready, n * M + (m + 1))
                        act.activation(f_head[:, m, :], fused[:, m % FUSED, :], ACT.Copy).then_inc(f_head_ready, 1)

        @block.vector
        def _(dve):
            count = [0]

            def step(ins):
                count[0] += 1
                ins.then_inc(dve_step, 1)
                dve.wait_ge(dve_step, count[0])

            def tile_stats(n, k, source):
                step(dve.bn_stats(stats[:, n, k, :], source[:, k, :]))
                dve.bn_aggr(mean_var[:, n, k, :], stats[:, n, k, :]).then_inc(stats_ready[n], 1)

            def normalise(n, b, ready):
                for k in range(T * b, T * b + T):
                    src = (x_in, x1, None, x3)[n]
                    dve.wait_ge(rstd_ready[n], k + 1)
                    dve.tensor_scalar(normed[:, k, :], src[:, k, :], mean_var[:, n, k, 0:1],
                                      rstd[:, n, k:k + 1], ALU.subtract, ALU.mult).then_inc(ready, 1)

            def first_stats(b):
                for k in range(T * b, T * b + T):
                    if k % 2 == 0:
                        dve.wait_ge(x_loaded[k // 2], 16)
                    tile_stats(0, k, x_in)

            first_stats(0)
            normalise(0, 0, z_ready)
            dve.wait_ge(w_turned_pe, 2)
            dve.tensor_copy(w_turned[:, 1, :, :].rearrange("p c n -> p (c n)"), psum[:, BANK_WT[1], :]).then_inc(wt_by_dve, 1)
            first_stats(1)

            def xn_chunk(b):
                dve.wait_ge(params_ready, 1)
                dve.wait_ge(z_turned, C * b + 2)
                dve.tensor_scalar(xn_cols[:, b, 1, :], psum[:, BANK_Z[b][1], :], gammas[:, 1:2], betas[:, 1:2],
                                  ALU.mult, ALU.add).then_inc(xn_by_dve, 1)

            def g_chunk(b):
                dve.wait_ge(g_made, C * b + 2)
                dve.tensor_scalar(g_cols[:, b, 1, :], psum[:, BANK_G[b][1], :], float(KEY) ** -0.5, None,
                                  ALU.mult).then_inc(g_by_dve, 1)

            def v_half(b):
                dve.wait_ge(v_made, 2 * b + 2)
                dve.tensor_copy(v_rows[:, b, 2:4, :].rearrange("p t n -> p (t n)"),
                                psum[:, BANK_V[b][1], :]).then_inc(v_by_dve, 1)

            W2 = HN + C
            st = lambda n, w=HN: s4d[:, n, 0:w]

            def exp_reduce():
                dve.wait_ge(s4d_loaded, 64)
                dve.tensor_copy(e_in[:, 0:HN], s4d_in[:, 0, :])
                step(dve.tensor_copy(e_in[:, HN:W2], log_dts))
                step(dve.tensor_scalar(st(0, W2), e_in[:], LOG2E, ROUND, ALU.mult, ALU.add))
                step(dve.tensor_scalar(st(0, W2), st(0, W2), -ROUND, None, ALU.add))
                step(dve.scalar_tensor_tensor(out=st(1, W2), in0=st(0, W2), scalar=-LN2_HI, in1=e_in[:], op0=ALU.mult, op1=ALU.add))
                step(dve.scalar_tensor_tensor(out=st(2, W2), in0=st(0, W2), scalar=-LN2_LO, in1=st(1, W2), op0=ALU.mult, op1=ALU.add))
                step(dve.tensor_scalar(st(4, W2), st(0, W2), -127.0, 128.0, ALU.max, ALU.min))
                dve.tensor_scalar(two_k[:], st(4, W2), 127.0, 2.0**23, ALU.add, ALU.mult).then_inc(tanh_in, 1)

            def exp_finish():
                dve.wait_ge(tanh_in, 1)
                dve.wait_ge(tanh_out, 1)
                step(dve.tensor_scalar(st(4, W2), st(3, W2), -1.0, 1.0, ALU.mult, ALU.add))
                step(dve.reciprocal(st(5, W2), st(4, W2)))
                step(dve.scalar_tensor_tensor(out=st(6, W2), in0=st(3, W2), scalar=1.0, in1=st(5, W2), op0=ALU.add, op1=ALU.mult))
                step(dve.tensor_tensor(st(7, W2), st(6, W2), two_k[:].bitcast(F32), ALU.mult))
                for c in range(C):
                    dt = s4d[:, 7, HN + c:HN + c + 1]
                    cs = slice(N * c, N * c + N)
                    dve.tensor_scalar(s4d[:, 8, cs], s4d[:, 7, cs], dt, -1.0, ALU.mult, ALU.mult)
                    step(dve.tensor_scalar(s4d[:, 13, cs], s4d_in[:, 1, cs], dt, None, ALU.mult))
                step(dve.tensor_scalar(st(14), st(13), 1.0 / (2.0 * np.pi), ROUND, ALU.mult, ALU.add))
                step(dve.tensor_scalar(st(14), st(14), -ROUND, None, ALU.add))
                for part in TWO_PI:
                    step(dve.scalar_tensor_tensor(out=st(13), in0=st(14), scalar=-part, in1=st(13), op0=ALU.mult, op1=ALU.add))
                dve.tensor_scalar(st(9), st(13), -PI_BELOW, PI_BELOW, ALU.max, ALU.min).then_inc(trig_in, 1)

            def taps_finish():
                w, cr, ci = s4d_in[:, 1, :], s4d_in[:, 2, :], s4d_in[:, 3, :]
                a = st(7)
                dve.wait_ge(trig_out, 1)
                step(dve.tensor_scalar(st(15), st(10), -1.0, 1.0, ALU.mult, ALU.add))
                step(dve.reciprocal(st(16), st(15)))
                step(dve.scalar_tensor_tensor(out=st(17), in0=st(10), scalar=2.0, in1=st(16), op0=ALU.mult, op1=ALU.mult))
                step(dve.tensor_scalar(st(18), st(17), 1.0, None, ALU.add))
                step(dve.scalar_tensor_tensor(out=st(19), in0=st(12), scalar=-2.0, in1=st(12), op0=ALU.mult, op1=ALU.mult))
                step(dve.tensor_tensor(st(20), st(18), st(19), ALU.mult))
                step(dve.tensor_tensor(st(21), st(20), st(17), ALU.add))
                step(dve.tensor_tensor(st(22), st(18), st(11), ALU.mult))
                step(dve.tensor_tensor(st(23), cr, st(21), ALU.mult))
                step(dve.tensor_tensor(st(24), ci, st(22), ALU.mult))
                step(dve.tensor_tensor(st(25), st(23), st(24), ALU.subtract))
                step(dve.tensor_tensor(st(23), cr, st(22), ALU.mult))
                step(dve.tensor_tensor(st(24), ci, st(21), ALU.mult))
                step(dve.tensor_tensor(st(26), st(23), st(24), ALU.add))
                step(dve.tensor_tensor(st(27), a, a, ALU.mult))
                step(dve.tensor_tensor(st(28), w, w, ALU.mult))
                step(dve.tensor_tensor(st(27), st(27), st(28), ALU.add))
                step(dve.reciprocal(st(29), st(27)))
                step(dve.tensor_tensor(st(30), st(25), a, ALU.mult))
                step(dve.tensor_tensor(st(31), st(26), w, ALU.mult))
                step(dve.tensor_tensor(st(32), st(31), st(30), ALU.subtract))
                step(dve.tensor_tensor(st(33), st(32), st(29), ALU.mult))
                step(dve.tensor_tensor(st(30), st(25), w, ALU.mult))
                step(dve.tensor_tensor(st(31), st(26), a, ALU.mult))
                step(dve.scalar_tensor_tensor(out=st(32), in0=st(30), scalar=-1.0, in1=st(31), op0=ALU.mult, op1=ALU.subtract))
                step(dve.tensor_tensor(st(34), st(32), st(29), ALU.mult))
                step(dve.scalar_tensor_tensor(out=st(35), in0=st(21), scalar=1.0, in1=st(33), op0=ALU.add, op1=ALU.mult))
                step(dve.tensor_tensor(st(36), st(34), st(22), ALU.mult))
                step(dve.tensor_tensor(st(37), st(35), st(36), ALU.subtract))
                dve.tensor_reduce(s4d[:, 38, 0:C], st(33).rearrange("p (c n) -> p c n", c=C), AX_X, ALU.add)
                step(dve.tensor_reduce(s4d[:, 39, 0:C], st(37).rearrange("p (c n) -> p c n", c=C), AX_X, ALU.add))
                dve.scalar_tensor_tensor(out=taps[:, 0, :], in0=s4d[:, 38, 0:C], scalar=2.0, in1=d_params, op0=ALU.mult, op1=ALU.add)
                dve.tensor_scalar(taps[:, 1, :], s4d[:, 39, 0:C], 2.0, None, ALU.mult).then_inc(taps_ready, 1)

            raws = (gate_raw, up_raw, down_raw)

            def weight_grid(w):
                dve.wait_ge(w_loaded[w], 16)
                flat = raws[w][:].rearrange("p c n -> p (c n)")
                dve.tensor_tensor_reduce(square[w][:], flat, flat, 1.0, 0.0, ALU.mult, ALU.max, max_square[:, w:w + 1])
                step(dve.tensor_scalar(grid[w][:].bitcast(U32), flat.bitcast(U32), 0x7F800000, None, ALU.bitwise_and))
                dve.tensor_scalar(grid[w][:], grid[w][:], 2.0**-6, 1.5 * 2.0**20, ALU.max, ALU.mult).then_inc(grid_ready, 1)

            def mark_beyond():
                dve.wait_ge(grid_ready, 3)
                step(dve.tensor_reduce(max_square[:, 3:4], max_square[:, 0:3], AX_X, ALU.max))
                dve.tensor_scalar(beyond[:, 0:1], max_square[:, 3:4], FP8_LARGEST**2, None, ALU.is_gt).then_inc(squares_ready, 1)

            def bound_gate_up():
                dve.wait_ge(norms_made, 1)
                dve.tensor_scalar(bound[:, 0, :], psum[:, BANK_NORMS, 0:M], 2.26, 5e-4, ALU.mult, ALU.add)
                dve.tensor_scalar(bound[:, 1, :], psum[:, BANK_NORMS, M:2 * M], 2.26, 5e-4, ALU.mult, ALU.add)
                step(dve.tensor_scalar(beyond[:, 1:2], psum[:, BANK_NORMS, 2 * M:2 * M + 1], 0.0, 3e38, ALU.is_gt, ALU.mult))
                norms_read_at = dve.tensor_scalar(beyond[:, 2:3], beyond[:, 1:2], 3e38, None, ALU.mult)
                norms_read_at.then_inc(norms_read, 1)
                step(dve.tensor_tensor(bound[:, 2, :], gate_scales, up_scales, ALU.mult))
                step(dve.tensor_tensor(bound[:, 2, :], bound[:, 2, :], bound[:, 2, :], ALU.mult))
                step(dve.tensor_tensor(bound[:, 1, :], bound[:, 1, :], bound[:, 0, :], ALU.mult))
                dve.scalar_tensor_tensor(out=bound[:, 3, :], in0=bound[:, 1, :], scalar=65536.0, in1=bound[:, 2, :],
                                         op0=ALU.mult, op1=ALU.mult).then_inc(bound_squared, 1)
                dve.wait_ge(norms_read, 1)
                step(dve.tensor_tensor(beyond[:, 3:4], beyond[:, 2:3], beyond[:, 2:3], ALU.subtract))
                dve.wait_ge(down_scale_loaded, 16)
                dve.tensor_scalar(down_scale_all[:], down_scale_all[:], beyond[:, 3:4], None, ALU.add)

            def fit_powers():
                dve.wait_ge(bound_ready, 1)
                step(dve.tensor_scalar(bound[:, 5, :].bitcast(U32), bound[:, 4, :].bitcast(U32), 0x7F800000, None, ALU.bitwise_and))
                step(dve.tensor_scalar(bound[:, 6, :], bound[:, 5, :], 2.0**-80, 2.0**-14, ALU.max, ALU.mult))
                step(dve.reciprocal(bound[:, 7, :], bound[:, 6, :]))
                dve.tensor_tensor(up_scales_fit[:], up_scales, bound[:, 7, :], ALU.mult).then_inc(fit_ready, 1)

            def row_max(k):
                dve.wait_ge(scores_made, k + 1)
                dve.tensor_reduce(neg_max[:, k:k + 1], psum[:, BANK_S[k % 2], 0:P * (k % T + 1)], AX_X, ALU.max,
                                  negate=True).then_inc(max_ready, 1)

            def attention_out(k):
                dve.wait_ge(probs_ready, k + 1)
                step(dve.reciprocal(inv_sum[:, k:k + 1], row_sum[:, k:k + 1]))
                dve.wait_ge(attn_made, k + 1)
                dve.wait_ge(x_plus_ready, k + 1)
                dve.scalar_tensor_tensor(out=x1[:, k, :], in0=psum[:, BANK_O[k % 2], 0:H], scalar=inv_sum[:, k:k + 1],
                                         in1=x_plus[:, k, :], op0=ALU.mult, op1=ALU.add).then_inc(x1_ready, 1)
                dve.wait_ge(x1_ready, k + 1)
                tile_stats(1, k, x1)

            dve.wait_ge(params_turned, 1)
            dve.tensor_copy(params[:], psum[:, BANK_PARAMS, 0:NR]).then_inc(params_ready, 1)
            xn_chunk(0)
            normalise(0, 1, z_ready)
            weight_grid(0)
            g_chunk(0)
            xn_chunk(1)
            exp_reduce()
            weight_grid(1)
            v_half(0)
            exp_finish()
            g_chunk(1)
            weight_grid(2)
            mark_beyond()
            v_half(1)
            for k in range(K + 2):
                if k < K:
                    row_max(k)
                if k >= 2:
                    attention_out(k - 2)
                if k == 4:
                    bound_gate_up()
                if k == 5:
                    fit_powers()
                if k == 7:
                    normalise(1, 0, h_ready)
            normalise(1, 1, h_ready)

            def ffn_scale(n, k):
                b, t = tile_of[k]
                dve.wait_ge(down_made, 2 * (B * n + b) + t // 2 + 1)
                dve.tensor_tensor(scaled_down[:, k, :], psum[:, BANK_DOWN[t // 2], H * (t % 2):H * (t % 2) + H],
                                  down_scale_all[:], ALU.mult).then_inc(down_read, 1)

            def x2_stats(k):
                dve.wait_ge(x2_ready, k + 1)
                tile_stats(2, k, x2)

            def s4d_mix(k):
                b, t = tile_of[k]
                dve.wait_ge(rstd_ready[2], k + 1)
                dve.wait_ge(taps_loaded, 16)
                step(dve.scalar_tensor_tensor(out=normed[:, k, :], in0=x2[:, k, :], scalar=mean_var[:, 2, k, 0:1],
                                              in1=taps_all[:, 0, :], op0=ALU.subtract, op1=ALU.mult))
                if b:
                    dve.wait_ge(lag_ready, t + 1)
                dve.scalar_tensor_tensor(out=x3[:, k, :], in0=normed[:, k, :], scalar=rstd[:, 2, k:k + 1],
                                         in1=x2_lag[:, t, :] if b else x2[:, k, :], op0=ALU.mult,
                                         op1=ALU.add).then_inc(x3_ready, 1)
                dve.wait_ge(x3_ready, k + 1)
                tile_stats(3, k, x3)

            def scale_pass(n, b):
                for k in range(T * b, T * b + T):
                    ffn_scale(n, k)

            def between(n, b, m):
                tiles = range(T * b, T * b + T)
                if n == 0:
                    if m == 1:
                        for k in tiles:
                            x2_stats(k)
                    if m == 3:
                        for k in list(tiles)[:2]:
                            s4d_mix(k)
                    if m == 4:
                        for k in list(tiles)[2:]:
                            s4d_mix(k)
                    if m == 5:
                        normalise(3, b, h_ready)

            for f in range(2):
                for b in range(B):
                    n = B * f + b
                    for c in range(C):
                        dve.wait_ge(h_head_ready, C * n + c + 1)
                        dve.tensor_tensor(h_tail[:, b, c, :], psum[:, BANK_H[c], :], h_head[:, b, c, :],
                                          ALU.subtract).then_inc(h_tail_ready, 1)
                    for m in range(M):
                        i = M * n + m
                        dve.wait_ge(gated_ready, i + 1)
                        dve.wait_ge(up_made, i + 1)
                        held = (m - FUSED) % M
                        if held in POOL_TAILS and i >= FUSED:
                            dve.wait_ge(f_tail_by_pool, len(POOL_TAILS) * ((i - FUSED) // M) + POOL_TAILS.index(held) + 1)
                        dve.scalar_tensor_tensor(out=fused[:, m % FUSED, :], in0=psum[:, BANK_UP[m % 2], :],
                                                 scalar=up_scales_fit[:, m:m + 1], in1=gated[:, m % 2, :],
                                                 op0=ALU.mult, op1=ALU.mult).then_inc(fused_ready, 1)
                        if n >= 1 and m == 0:
                            scale_pass((n - 1) // B, (n - 1) % B)
                        if m in DVE_TAILS:
                            dve.wait_ge(f_head_ready, i + 1)
                            dve.tensor_tensor(f_tail[:, m, :], fused[:, m % FUSED, :], f_head[:, m, :],
                                              ALU.subtract).then_inc(f_tail_by_dve, 1)
                        if n == 0 and m == 0:
                            taps_finish()
                        if n >= 1:
                            between((n - 1) // B, (n - 1) % B, m)
            scale_pass(1, 1)

        @block.tensor
        def _(pe):
            def column(bank, start, width):
                return psum[:, bank, start:start + width]

            pe.wait_ge(ident_ready, 1)
            for n in range(WARM_UP):
                pe.transpose(column(BANK_NORMS, 0, P), ident[:], ident[:])

            def turn_w(w, loaded):
                pe.wait_ge(loaded, 16)
                for kc in range(C):
                    for c in range(C):
                        last = pe.transpose(column(BANK_WT[w], kc * H + c * P, P),
                                            qkv_sb[:, c, w * KEY + kc * P:w * KEY + kc * P + P], ident[:])
                last.then_inc(w_turned_pe, 1)

            def fold(bank, left, right):
                for c in range(C):
                    for kc in range(C):
                        last = pe.matmul(column(bank, c * H, H), w_turned[:, left, kc, c * P:c * P + P], right(kc),
                                         start=(kc == 0), stop=(kc == C - 1))
                return last

            def turn_z(b):
                for c in range(C):
                    for t in range(T):
                        if c == 0:
                            pe.wait_ge(z_ready, T * b + t + 1)
                        last = pe.transpose(column(BANK_Z[b][c], t * P, P), normed[:, T * b + t, c * P:c * P + P], ident[:])
                    last.then_inc(z_turned, 1)

            def make_g(b):
                pe.wait_ge(xn_by_act, b + 1)
                pe.wait_ge(xn_by_dve, b + 1)
                for j in range(C):
                    for c in range(C):
                        last = pe.matmul(column(BANK_G[b][j], 0, S), wqk[:, c, j * P:j * P + P], xn_cols[:, b, c, :],
                                         start=(c == 0), stop=(c == C - 1))
                    last.then_inc(g_made, 1)

            def make_v(b):
                for t in range(T):
                    for c in range(C):
                        last = pe.matmul(column(BANK_V[b][t // 2], H * (t % 2), H), xn_cols[:, b, c, t * P:t * P + P],
                                         wvo[:, c, :], start=(c == 0), stop=(c == C - 1))
                    if t % 2:
                        last.then_inc(v_made, 1)

            turn_w(0, qk_loaded)
            turn_w(1, qk_loaded)
            turn_z(0)
            pe.wait_ge(wt_by_act, 1)
            pe.wait_ge(wt_by_dve, 1)
            fold(BANK_WQK, 0, lambda kc: w_turned[:, 1, kc, :]).then_inc(wqk_made, 1)
            pe.wait_ge(rows_loaded, 96)
            pe.transpose(column(BANK_PARAMS, 0, NR), param_rows[:], ident[0:NR, 0:NR]).then_inc(params_turned, 1)
            turn_w(2, v_loaded)
            pe.wait_ge(wqk_ready, 1)
            pe.wait_ge(params_ready, 1)
            make_g(0)
            pe.wait_ge(wt_by_act, 2)
            pe.wait_ge(wo_loaded, 16)
            fold(BANK_WVO, 2, lambda kc: wo_sb[:, kc, :]).then_inc(wvo_made, 1)
            turn_z(1)
            pe.wait_ge(wvo_ready, 1)
            make_v(0)
            make_g(1)
            make_v(1)

            def scores(k):
                b, i = tile_of[k]
                if k == 0:
                    pe.wait_ge(consts_ready, 1)
                    pe.wait_ge(g_by_act, 1)
                    pe.wait_ge(g_by_dve, 1)
                if k == T:
                    pe.wait_ge(g_by_act, 2)
                    pe.wait_ge(g_by_dve, 2)
                if k >= 2:
                    pe.wait_ge(probs_ready, k - 1)
                W = P * (i + 1)
                for j in range(C):
                    pe.matmul(column(BANK_S[k % 2], 0, W), g_cols[:, b, j, i * P:i * P + P], xn_cols[:, b, j, 0:W],
                              start=(j == 0), stop=(j == C - 1))
                pe.matmul(column(BANK_S[k % 2], i * P, P), ident16[:], mask[:], start=False, stop=True,
                          skip_group_check=True).then_inc(scores_made, 1)

            def turn_probs(k):
                pe.wait_ge(probs_ready, k + 1)
                if k == 0:
                    pe.wait_ge(v_by_act, 1)
                    pe.wait_ge(v_by_dve, 1)
                if k >= 2:
                    pe.wait_ge(probs_cols_ready, k - 1)
                for t in range(k % T + 1):
                    last = pe.transpose(column(BANK_PT[k % 2], t * P, P), probs[:, k % 2, t * P:t * P + P], ident[:])
                last.then_inc(probs_turned, 1)

            def attend(k):
                b, i = tile_of[k]
                pe.wait_ge(probs_cols_ready, k + 1)
                if k == T:
                    pe.wait_ge(v_by_act, 2)
                    pe.wait_ge(v_by_dve, 2)
                if k >= 2:
                    pe.wait_ge(x1_ready, k - 1)
                for t in range(i + 1):
                    last = pe.matmul(column(BANK_O[k % 2], 0, H), probs_cols[:, k % 2, t * P:t * P + P],
                                     v_rows[:, b, t, :], start=(t == 0), stop=(t == i))
                last.then_inc(attn_made, 1)

            def channel_norms():
                pe.wait_ge(squares_ready, 1)
                pe.wait_ge(v_by_dve, 2)
                for w in range(2):
                    for m in range(M):
                        for c in range(C):
                            pe.matmul(column(BANK_NORMS, M * w + m, 1), square[w][:, c * I + m * P:c * I + m * P + P],
                                      ones16[:, 0:1], start=(c == 0), stop=(c == C - 1))
                pe.matmul(column(BANK_NORMS, 2 * M, 1), ones[:], beyond[:, 0:1], start=True,
                          stop=True).then_inc(norms_made, 1)

            for k in range(K + 2):
                if k < K:
                    scores(k)
                if 1 <= k <= K:
                    turn_probs(k - 1)
                if k == 3:
                    channel_norms()
                if k >= 2:
                    attend(k - 2)

            pe.wait_ge(norms_read, 1)
            pe.wait_ge(gate_up_ready, 2)
            with pe.Fori(0, 2) as f:
                def turn_h(b):
                    n = f * B + b
                    pe.wait_ge(h_ready, n * T + T)
                    if b:
                        pe.wait_ge(h_tail_ready, n * C)
                    for c in range(C):
                        for t in range(T):
                            last = pe.transpose(column(BANK_H[c], t * P, P), normed[:, T * b + t, c * P:c * P + P], ident[:])
                        last.then_inc(h_turned, 1)

                def gate_up(b, m):
                    n = f * B + b
                    for w, banks, made, read in ((gate16, BANK_GATE, gate_made, gated_ready), (up16, BANK_UP, up_made, fused_ready)):
                        if (b, m) >= (0, 2):
                            pe.wait_ge(read, n * M + m - 1)
                        for part, ready in ((h_head, h_head_ready), (h_tail, h_tail_ready)):
                            for c in range(C):
                                if m == 0 and w is gate16:
                                    pe.wait_ge(ready, n * C + (c + 1))
                                last = pe.matmul(column(banks[m % 2], 0, S), w[:, c, m * P:m * P + P], part[:, b, c, :],
                                                 start=(part is h_head and c == 0), stop=(part is h_tail and c == C - 1))
                        last.then_inc(made, 1)

                def down(b, m):
                    n = f * B + b
                    if m in POOL_TAILS:
                        pe.wait_ge(f_tail_by_pool, n * len(POOL_TAILS) + (POOL_TAILS.index(m) + 1))
                    else:
                        pe.wait_ge(f_tail_by_dve, n * len(DVE_TAILS) + (DVE_TAILS.index(m) + 1))
                    if b == 0:
                        pe.wait_ge(down_ready, m + 1)
                    for t in range(T):
                        for part in (f_head, f_tail):
                            last = pe.matmul(column(BANK_DOWN[t // 2], H * (t % 2), H), part[:, m, t * P:t * P + P],
                                             down16[:, m, :], start=(m == 0 and t % 2 == 0 and part is f_head),
                                             stop=(m == M - 1 and part is f_tail), skip_group_check=True)
                        if m == M - 1 and t % 2:
                            last.then_inc(down_made, 1)

                turn_h(0)
                for b in range(B):
                    for m in range(M):
                        gate_up(b, m)
                        if m >= 2:
                            down(b, m - 2)
                    if b + 1 < B:
                        turn_h(b + 1)
                    down(b, M - 2)
                    down(b, M - 1)


_INS = ['x', 'qkv', 'o_proj', 'gamma', 'beta', 'd_param', 'log_dt', 'a_real_log', 'a_imag', 'c_re', 'c_im',
        'gate_w', 'up_w', 'down_w', 'gate_scale', 'up_scale', 'down_scale']


def kernel(L0_attn_a_x, L0_attn_a_qkv, L0_attn_a_o_proj, L0_attn_a_gamma, L0_attn_a_beta, L0_attn_b_D_param,
           L0_attn_b_log_dt, L0_attn_b_A_real_log, L0_attn_b_A_imag, L0_attn_b_C_re, L0_attn_b_C_im, L0_ffn_gate_w,
           L0_ffn_up_w, L0_ffn_down_w, L0_ffn_gate_scale, L0_ffn_up_scale, L0_ffn_down_scale):
    import concourse.bacc as bacc
    from concourse.bass_utils import run_bass_kernel_spmd

    given = (L0_attn_a_x, L0_attn_a_qkv, L0_attn_a_o_proj, L0_attn_a_gamma, L0_attn_a_beta, L0_attn_b_D_param,
             L0_attn_b_log_dt, L0_attn_b_A_real_log, L0_attn_b_A_imag, L0_attn_b_C_re, L0_attn_b_C_im, L0_ffn_gate_w,
             L0_ffn_up_w, L0_ffn_down_w, L0_ffn_gate_scale, L0_ffn_up_scale, L0_ffn_down_scale)
    nc = bacc.Bacc("TRN2", target_bir_lowering=False, num_devices=1)
    arrays, aps = {}, []
    for name, value in zip(_INS, given):
        array = np.ascontiguousarray(value)
        arrays[f"in_{name}"] = array
        aps.append(nc.dram_tensor(f"in_{name}", array.shape, mybir.dt.from_np(array.dtype), kind="ExternalInput").ap())
    out = nc.dram_tensor("out", arrays["in_x"].shape, F32, kind="ExternalOutput").ap()
    hybrid_layer(nc, *aps, out)
    result = run_bass_kernel_spmd(nc, [arrays], core_ids=[0])
    return result.results[0]["out"]
```

```python
from contextlib import ExitStack

import numpy as np

import concourse.bass as bass
from concourse import mybir

F32 = mybir.dt.float32
F16 = mybir.dt.float16
BF16 = mybir.dt.bfloat16
U32 = mybir.dt.uint32
I32 = mybir.dt.int32
ALU = mybir.AluOpType
ACT = mybir.ActivationFunctionType
AX_X = mybir.AxisListType.X

P = 128
EPS = 1e-5
MASKED = -3.0e38
WARM_UP = 14
ROUND = 1.5 * 2.0**23
FP8_LARGEST = 464.0
LOG2E = float(np.float32(np.log2(np.e)))
LN2_HI = 0.693145751953125
LN2_LO = float(np.log(2.0) - LN2_HI)
TWO_PI = [6.28125, 0.0019340515136718750, float(2 * np.pi - 6.28125 - 0.0019340515136718750)]
PI_BELOW = float(np.nextafter(np.float32(np.pi), np.float32(0)))


def hybrid_layer(nc, x, qkv, o_proj, gamma, beta, d_param, log_dt, a_real_log, a_imag, c_re, c_im,
                 gate_w, up_w, down_w, gate_scale, up_scale, down_scale, out):
    B, S, H = x.shape
    KEY = qkv.shape[1] // 3
    I = gate_w.shape[1]
    N = a_imag.shape[1]
    T = S // P
    C = H // P
    M = I // P
    K = B * T
    HN = C * N
    assert KEY == H and C == 2 and T == 4 and B == 2 and H * 2 == 512

    ctx = ExitStack()
    with ctx:
        def sb(name, shape, dt=F32):
            return ctx.enter_context(nc.sbuf_tensor(name, shape, dt))

        def sem(name):
            return ctx.enter_context(nc.semaphore(name))

        x_in = sb("x_in", [P, K, H])
        x_plus = sb("x_plus", [P, K, H])
        x1 = sb("x1", [P, K, H])
        x2 = sb("x2", [P, K, H])
        x3 = x_plus
        x4 = x_in
        normed = sb("normed", [P, K, H])
        h_rows = sb("h_rows", [P, T, H])
        scaled_down = sb("scaled_down", [P, K, H])
        qkv_sb = sb("qkv_sb", [P, C, 3 * KEY])
        wo_sb = sb("wo_sb", [P, C, H])
        w_turned = sb("w_turned", [P, 3, C, H])
        wqk = sb("wqk", [P, C, H])
        wvo = sb("wvo", [P, C, H])
        xn_cols = sb("xn_cols", [P, B, C, S])
        g_cols = sb("g_cols", [P, B, C, S])
        v_rows = sb("v_rows", [P, B, T, H])
        probs = sb("probs", [P, 2, S])
        probs_cols = sb("probs_cols", [P, 2, S])
        neg_max = sb("neg_max", [P, K])
        row_sum = sb("row_sum", [P, K])
        inv_sum = sb("inv_sum", [P, K])
        gate_raw = sb("gate_raw", [P, C, I])
        up_raw = sb("up_raw", [P, C, I])
        down_raw = sb("down_raw", [P, M, H])
        grid = [sb(f"grid{w}", [P, C * I]) for w in range(3)]
        square = [sb(f"square{w}", [P, C * I], BF16) for w in range(3)]
        gate16 = sb("gate16", [P, C, I], F16)
        up16 = sb("up16", [P, C, I], F16)
        down_q = down_raw
        down16 = sb("down16", [P, M, H], BF16)
        max_square = sb("max_square", [P, 4])
        beyond = sb("beyond", [P, 4])
        down_scale_all = sb("down_scale_all", [P, H])
        ident = sb("ident", [P, P])
        ident16 = sb("ident16", [P, P], BF16)
        ones = sb("ones", [P, P])
        ones16 = sb("ones16", [P, 2], BF16)
        mask = sb("mask", [P, P], BF16)
        neg_half = sb("neg_half", [P, K])
        pos_half = sb("pos_half", [P, M])
        param_rows = sb("param_rows", [4 * C, P])
        params = sb("params", [P, 4 * C])
        gammas, betas, log_dts, d_params = (params[:, C * n:C * n + C] for n in range(4))
        scale_rows = sb("scale_rows", [2 * M, P])
        scales = sb("scales", [P, 2 * M])
        gate_scales, up_scales = scales[:, 0:M], scales[:, M:2 * M]
        stats = sb("stats", [P, 4, K, 6])
        mean_var = sb("mean_var", [P, 4, K, 2])
        var_eps = sb("var_eps", [P, 5, K])
        rstd = sb("rstd", [P, 5, K])
        one_rstd = sb("one_rstd", [P, K])
        mean_rstd = sb("mean_rstd", [P, 4, K])
        neg_mean_rstd = sb("neg_mean_rstd", [P, 4, K])
        bound = sb("bound", [P, 8, M])
        up_scales_fit = sb("up_scales_fit", [P, M])
        h_head = sb("h_head", [P, C, S], F16)
        h_tail = sb("h_tail", [P, C, S], F16)
        silu_table = sb("silu_table", [P, 1])
        gated = sb("gated", [P, 2, S])
        FUSED = 4
        fused = sb("fused", [P, FUSED, S])
        f_head = sb("f_head", [P, M, S], F16)
        f_tail = sb("f_tail", [P, M, S], F16)
        s4d_in = sb("s4d_in", [P, 4, HN])
        e_in = sb("e_in", [P, HN + C])
        s4d = sb("s4d", [P, 40, HN + C])
        two_k = sb("two_k", [P, HN + C], I32)
        taps = sb("taps", [P, 2, C])
        taps_all = sb("taps_all", [P, 2, H])
        x_lag = sb("x_lag", [P, T, H])
        x2_lag = sb("x2_lag", [P, T, H])
        psum = ctx.enter_context(nc.psum_tensor("psum", [P, 8, 512], F32))
        taps_dram = nc.dram_tensor("taps_dram", (2, H), F32)

        x_loaded = [sem(f"x_loaded{n}") for n in range(K // 2)]
        q_loaded, k_loaded, v_loaded, wo_loaded = sem("q_loaded"), sem("k_loaded"), sem("v_loaded"), sem("wo_loaded")
        params_loaded, scales_loaded = sem("params_loaded"), sem("scales_loaded")
        a_loaded, c_loaded = sem("a_loaded"), sem("c_loaded")
        w_loaded = [sem("gate_loaded"), sem("up_loaded"), sem("down_loaded")]
        down_scale_loaded = sem("down_scale_loaded")
        taps_stored, taps_loaded, out_stored = sem("taps_stored"), sem("taps_loaded"), sem("out_stored")
        pool_step = sem("pool_step")
        ident_ready, consts_ready = sem("ident_ready"), sem("consts_ready")
        params_turned, params_ready = sem("params_turned"), sem("params_ready")
        scales_turned, scales_ready = sem("scales_turned"), sem("scales_ready")
        dve_step = sem("dve_step")
        stats_ready = [sem(f"stats_ready{n}") for n in range(4)]
        rstd_ready = [sem(f"rstd_ready{n}") for n in range(4)]
        shift_ready = [None] + [sem(f"shift_ready{n}") for n in (1, 2, 3)]
        z2_ready = sem("z2_ready")
        z_ready, z_turned = sem("z_ready"), sem("z_turned")
        xn_by_act, xn_by_dve = sem("xn_by_act"), sem("xn_by_dve")
        w_turned_pe, w_turned_ready = sem("w_turned_pe"), sem("w_turned_ready")
        wqk_made, wvo_made, wqk_ready, wvo_ready = sem("wqk_made"), sem("wvo_made"), sem("wqk_ready"), sem("wvo_ready")
        g_made, g_by_act, g_by_dve = sem("g_made"), sem("g_by_act"), sem("g_by_dve")
        v_made, v_by_act, v_by_dve = sem("v_made"), sem("v_by_act"), sem("v_by_dve")
        x_plus_ready = sem("x_plus_ready")
        scores_made, max_ready, probs_ready = sem("scores_made"), sem("max_ready"), sem("probs_ready")
        probs_turned, probs_cols_ready = sem("probs_turned"), sem("probs_cols_ready")
        attn_made, x1_ready = sem("attn_made"), sem("x1_ready")
        squares_ready, norms_made, norms_read = sem("squares_ready"), sem("norms_made"), sem("norms_read")
        fit_ready, bound_squared, bound_ready = sem("fit_ready"), sem("bound_squared"), sem("bound_ready")
        grid_ready, gate_up_ready, down_ready = sem("grid_ready"), sem("gate_up_ready"), sem("down_ready")
        h_ready = [sem("h_first_ready"), sem("h_second_ready")]
        h_turned, h_head_ready, h_tail_ready = sem("h_turned"), sem("h_head_ready"), sem("h_tail_ready")
        gate_made, up_made, gated_ready = sem("gate_made"), sem("up_made"), sem("gated_ready")
        fused_ready, f_head_ready = sem("fused_ready"), sem("f_head_ready")
        f_tail_by_pool, f_tail_by_dve = sem("f_tail_by_pool"), sem("f_tail_by_dve")
        down_made, down_read = sem("down_made"), sem("down_read")
        x2_by_pool, x2_by_dve, x3_ready, lag_ready, x4_by_pool, x4_by_dve = sem("x2_by_pool"), sem("x2_by_dve"), sem("x3_ready"), sem("lag_ready"), sem("x4_by_pool"), sem("x4_by_dve")
        tanh_in, tanh_out, trig_in, trig_out, magnitude_ready, taps_ready = sem("tanh_in"), sem("tanh_out"), sem("trig_in"), sem("trig_out"), sem("magnitude_ready"), sem("taps_ready")

        POOL_TAILS = (1, 3, 4)
        DVE_TAILS = tuple(m for m in range(M) if m not in POOL_TAILS)

        BANK_WT, BANK_WQK, BANK_WVO, BANK_PARAMS, BANK_SCALES, BANK_NORMS = [4, 5, 3], 2, 3, 7, 4, 5
        BANK_Z = [[0, 1], [4, 5]]
        BANK_G = [[6, 7], [0, 1]]
        BANK_V = [[2, 3], [4, 5]]
        BANK_S, BANK_PT, BANK_O = [6, 7], [2, 3], [0, 1]
        raws = (gate_raw, up_raw, down_raw)

        def flat(tensor):
            return tensor[:].rearrange("p c n -> p (c n)")

        BANK_H, BANK_GATE, BANK_UP, BANK_DOWN = [4, 5], [6, 2], [7, 3], [0, 1]

        x_tiles = x.rearrange("b (t p) h -> p (b t) h", p=P)
        out_tiles = out.rearrange("b (t p) h -> p (b t) h", p=P)
        tile_of = [(b, t) for b in range(B) for t in range(T)]

        block = ctx.enter_context(nc.Block())

        @block.sync
        def _(sp):
            def load_x(n):
                sp.dma_start(x_in[:, 2 * n:2 * n + 2, :], x_tiles[:, 2 * n:2 * n + 2, :]).then_inc(x_loaded[n], 16)

            def load_chunks(to, array, loaded):
                sp.dma_start(to, array.rearrange("(c p) n -> p c n", p=P)).then_inc(loaded, 16)

            def load_rows(to, vectors, loaded):
                at = 0
                for vector in vectors:
                    n = vector.shape[0] // P
                    sp.dma_start(to[at:at + n, :], vector.rearrange("(m p) -> m p", p=P)).then_inc(loaded, 16)
                    at += n

            load_x(0)
            load_chunks(qkv_sb[:, :, 0:KEY], qkv[:, 0:KEY], q_loaded)
            load_x(1)
            load_chunks(qkv_sb[:, :, KEY:2 * KEY], qkv[:, KEY:2 * KEY], k_loaded)
            load_rows(param_rows, (gamma, beta, log_dt, d_param), params_loaded)
            load_chunks(qkv_sb[:, :, 2 * KEY:], qkv[:, 2 * KEY:], v_loaded)
            load_x(2)
            load_x(3)
            load_chunks(wo_sb[:], o_proj, wo_loaded)
            load_rows(scale_rows, (gate_scale, up_scale), scales_loaded)
            load_chunks(gate_raw[:], gate_w, w_loaded[0])
            load_chunks(up_raw[:], up_w, w_loaded[1])
            load_chunks(down_raw[:], down_w, w_loaded[2])
            sp.dma_start(down_scale_all[:], down_scale.partition_broadcast(P)).then_inc(down_scale_loaded, 16)
            sp.wait_ge(taps_ready, 1)
            with nc.allow_non_contiguous_dma(reason="256 taps, one per partition"):
                for k in range(2):
                    sp.dma_start(taps_dram.ap()[k].rearrange("(c p) -> p c", p=P), taps[:, k, :]).then_inc(taps_stored, 16)
            sp.wait_ge(taps_stored, 32)
            sp.dma_start(taps_all[:], taps_dram.ap().partition_broadcast(P)).then_inc(taps_loaded, 16)
            def store(tiles):
                sp.dma_start(out_tiles[:, tiles, :], x4[:, tiles, :]).then_inc(out_stored, 16)

            for k in (0, 2):
                sp.wait_ge(x4_by_pool, k + 2)
                store(slice(k, k + 2))
            for t in (0, 2):
                sp.wait_ge(x4_by_pool, T + t // 2 + 1)
                sp.wait_ge(x4_by_dve, t // 2 + 1)
                store(slice(T + t, T + t + 2))
            sp.wait_ge(out_stored, 16 * (K // 2))

        @block.gpsimd
        def _(pool):
            count = [0]

            def step(ins):
                count[0] += 1
                ins.then_inc(pool_step, 1)
                pool.wait_ge(pool_step, count[0])

            step(pool.memset(ident[:], 0.0))
            pool.affine_select(out=ident[:], in_=ident[:], compare_op=ALU.not_equal, fill=1.0, base=0,
                               pattern=[[-1, P]], channel_multiplier=1).then_inc(ident_ready, 1)
            step(pool.memset(neg_half[:], -0.5))

            def load_s4d(n, array, loaded):
                pool.dma_start(s4d_in[:, n, :].rearrange("p (c n) -> p c n", c=C),
                               array.rearrange("(c p) n -> p c n", p=P)).then_inc(loaded, 16)

            load_s4d(0, a_real_log, a_loaded)
            load_s4d(1, a_imag, a_loaded)

            def inverse_std(n, k, count=1, twice=False, negative_mean=False):
                pool.wait_ge(stats_ready[n], k + count)
                factor, eps = (1.0 + EPS, EPS * EPS) if twice else (1.0, EPS)
                step(pool.tensor_scalar(var_eps[:, n, k:k + count], mean_var[:, n, k:k + count, 1], factor, eps, ALU.mult, ALU.add))
                power = pool.tensor_tensor(rstd[:, n, k:k + count], var_eps[:, n, k:k + count], neg_half[:, 0:count], ALU.pow)
                power.then_inc(rstd_ready[n], count)
                if not negative_mean:
                    return
                step(pool.tensor_scalar(mean_rstd[:, n, k:k + count], mean_var[:, n, k:k + count, 0], -1.0, 1.0,
                                        ALU.mult, ALU.mult))
                pool.wait_ge(rstd_ready[n], k + count)
                pool.tensor_tensor(neg_mean_rstd[:, n, k:k + count], mean_rstd[:, n, k:k + count],
                                   rstd[:, n, k:k + count], ALU.mult).then_inc(shift_ready[n], count)

            def mark(ins):
                count[0] += 1
                ins.then_inc(pool_step, 1)

            def settle():
                pool.wait_ge(pool_step, count[0])

            def make_taps():
                at = lambda n: s4d[:, n, 0:HN]
                w, cr, ci, a = s4d_in[:, 1, :], s4d_in[:, 2, :], s4d_in[:, 3, :], at(7)

                def product(n, left, right, op=ALU.mult):
                    mark(pool.tensor_tensor(at(n), left, right, op))

                pool.wait_ge(c_loaded, 32)
                pool.wait_ge(magnitude_ready, 1)
                pool.wait_ge(trig_out, 1)
                mark(pool.tensor_scalar(at(18), at(17), 1.0, 1.0, ALU.add, ALU.mult))
                product(19, at(12), at(12))
                settle()
                mark(pool.tensor_scalar(at(19), at(19), -2.0, 1.0, ALU.mult, ALU.mult))
                product(22, at(18), at(11))
                settle()
                product(20, at(18), at(19))
                product(24, ci, at(22))
                settle()
                product(21, at(20), at(17), ALU.add)
                product(23, cr, at(22))
                settle()
                product(25, cr, at(21))
                product(26, ci, at(21))
                mark(pool.tensor_scalar(at(35), at(21), 1.0, 1.0, ALU.add, ALU.mult))
                settle()
                product(25, at(25), at(24), ALU.subtract)
                product(26, at(23), at(26), ALU.add)
                settle()
                product(30, at(25), a)
                product(31, at(26), w)
                product(33, at(25), w)
                product(34, at(26), a)
                settle()
                product(32, at(31), at(30), ALU.subtract)
                product(34, at(33), at(34), ALU.add)
                settle()
                product(33, at(32), at(29))
                product(34, at(34), at(29))
                settle()
                product(35, at(35), at(33))
                product(36, at(34), at(22))
                settle()
                product(37, at(35), at(36), ALU.add)
                settle()
                parts = [s4d[:, n, 0:HN].rearrange("p (c n) -> p c n", c=C) for n in (33, 37)]
                width = N
                while width > 1:
                    width //= 2
                    for part in parts:
                        mark(pool.tensor_tensor(part[:, :, 0:width], part[:, :, 0:width], part[:, :, width:2 * width], ALU.add))
                    settle()
                mark(pool.tensor_scalar(s4d[:, 38, 0:C], parts[0][:, :, 0], 2.0, 1.0, ALU.mult, ALU.mult))
                settle()
                pool.tensor_tensor(taps[:, 0, :], s4d[:, 38, 0:C], d_params, ALU.add)
                pool.tensor_scalar(taps[:, 1, :], parts[1][:, :, 0], 2.0, 1.0, ALU.mult, ALU.mult).then_inc(taps_ready, 1)

            for k in range(0, K, 2):
                inverse_std(0, k, 2, twice=True)
                if k == T - 2:
                    load_s4d(2, c_re, c_loaded)
                    load_s4d(3, c_im, c_loaded)
                    pool.memset(pos_half[:], 0.5)
                    pool.memset(ones16[:], 1.0)
                    pool.memset(ones[:], 1.0)
                    step(pool.memset(mask[:], 0.0))
                    pool.affine_select(out=mask[:], in_=mask[:], compare_op=ALU.is_ge, fill=MASKED, base=0,
                                       pattern=[[-1, P]], channel_multiplier=1)
                    pool.tensor_copy(ident16[:], ident[:]).then_inc(consts_ready, 1)

            step(pool.tensor_scalar(var_eps[:, 4, :], mean_var[:, 0, :, 1], EPS, 1.0, ALU.add, ALU.mult))
            step(pool.tensor_tensor(rstd[:, 4, :], var_eps[:, 4, :], neg_half[:], ALU.pow))
            pool.tensor_scalar(one_rstd[:], rstd[:, 4, :], 1.0, 1.0, ALU.add, ALU.mult)
            step(pool.tensor_tensor(mean_rstd[:, 0, :], mean_var[:, 0, :, 0], rstd[:, 4, :], ALU.mult))
            step(pool.tensor_scalar(neg_mean_rstd[:, 0, :], mean_rstd[:, 0, :], -1.0, 1.0, ALU.mult, ALU.mult))
            for k in range(K):
                pool.tensor_scalar(x_plus[:, k, :], x_in[:, k, :], one_rstd[:, k:k + 1],
                                   neg_mean_rstd[:, 0, k:k + 1], ALU.mult, ALU.add).then_inc(x_plus_ready, 1)

            make_taps()

            def add_grid(w):
                pool.wait_ge(grid_ready, w + 1)
                return pool.tensor_tensor(flat(raws[w]), flat(raws[w]), grid[w][:], ALU.add)

            for w, rounded in ((0, gate16), (1, up16)):
                step(add_grid(w))
                pool.tensor_tensor(flat(rounded), flat(raws[w]), grid[w][:], ALU.subtract).then_inc(gate_up_ready, 1)
            inverse_std(1, 0, 2, negative_mean=True)
            inverse_std(1, 2, 2, negative_mean=True)
            mark(add_grid(2))
            pool.wait_ge(bound_squared, 1)
            pool.tensor_tensor(bound[:, 4, :], bound[:, 3, :], pos_half[:], ALU.pow).then_inc(bound_ready, 1)
            settle()
            step(pool.tensor_tensor(flat(down_q), flat(down_raw), grid[2][:], ALU.subtract))
            pool.wait_ge(fit_ready, 1)
            for m in range(M):
                pool.tensor_scalar(down16[:, m, :], down_q[:, m, :], bound[:, 6, m:m + 1], 1.0, ALU.mult,
                                   ALU.mult).then_inc(down_ready, 1)
            for k in range(T, K, 2):
                inverse_std(1, k, 2, negative_mean=True)

            def tail(n, m):
                pool.wait_ge(f_head_ready, M * n + m + 1)
                pool.tensor_tensor(f_tail[:, m, :], fused[:, m % FUSED, :], f_head[:, m, :],
                                   ALU.subtract).then_inc(f_tail_by_pool, 1)

            def residual(n, new, old, tiles, ready):
                for k in tiles:
                    pool.wait_ge(down_read, K * n + k + 1)
                    pool.tensor_tensor(new[:, k, :], scaled_down[:, k, :], old[:, k, :], ALU.add).then_inc(ready, 1)

            def lag_tap():
                pool.wait_ge(taps_loaded, 16)
                for t in range(T):
                    pool.wait_ge(z2_ready, t + 1)
                    mark(pool.tensor_tensor(x_lag[:, t, :], x_lag[:, t, :], taps_all[:, 1, :], ALU.mult))

            def add_lag(t):
                pool.tensor_tensor(x2_lag[:, t, :], x2[:, T + t, :], x_lag[:, t, :], ALU.add).then_inc(lag_ready, 1)

            for n in range(2 * B):
                first = T * (n - 1)
                if n in (1, 2):
                    residual(0, x2, x1, (first, first + 2, first + 3), x2_by_pool)
                    inverse_std(2, first, 2, negative_mean=(n == 1))
                    if n == 1:
                        tail(n, POOL_TAILS[0])
                    else:
                        settle()
                        add_lag(0)
                        add_lag(1)
                    inverse_std(2, first + 2, 2, negative_mean=(n == 1))
                    if n == 2:
                        add_lag(2)
                        add_lag(3)
                        tail(n, POOL_TAILS[0])
                    inverse_std(3, first, 2, negative_mean=True)
                    tail(n, POOL_TAILS[1])
                    inverse_std(3, first + 2, 2)
                    tail(n, POOL_TAILS[2])
                    if n == 1:
                        lag_tap()
                else:
                    tail(n, POOL_TAILS[0])
                    if n == 3:
                        residual(1, x4, x3, range(T), x4_by_pool)
                    tail(n, POOL_TAILS[1])
                    tail(n, POOL_TAILS[2])
            residual(1, x4, x3, (T, T + 2), x4_by_pool)

        @block.scalar
        def _(act):
            def turned(w):
                act.wait_ge(w_turned_pe, w + 1)
                act.activation(w_turned[:, w, :, :].rearrange("p c n -> p (c n)"), psum[:, BANK_WT[w], :],
                               ACT.Copy).then_inc(w_turned_ready, 1)

            def xn_chunk(b):
                act.wait_ge(params_ready, 1)
                act.wait_ge(z_turned, C * b + 1)
                act.activation(xn_cols[:, b, 0, :], psum[:, BANK_Z[b][0], :], ACT.Identity, scale=gammas[:, 0:1],
                               bias=betas[:, 0:1]).then_inc(xn_by_act, 1)

            def g_part(b):
                act.wait_ge(g_made, C * b + 1)
                act.activation(g_cols[:, b, 0, :], psum[:, BANK_G[b][0], :], ACT.Copy,
                               scale=float(KEY) ** -0.5).then_inc(g_by_act, 1)

            def v_part(b):
                act.wait_ge(v_made, 2 * b + 1)
                act.activation(v_rows[:, b, 0:2, :].rearrange("p t n -> p (t n)"), psum[:, BANK_V[b][0], :],
                               ACT.Copy).then_inc(v_by_act, 1)

            turned(0)
            turned(1)
            xn_chunk(0)
            act.wait_ge(wqk_made, 1)
            act.activation(wqk[:].rearrange("p c n -> p (c n)"), psum[:, BANK_WQK, :], ACT.Copy).then_inc(wqk_ready, 1)
            act.wait_ge(tanh_in, 1)
            act.activation(s4d[:, 3, :], s4d[:, 2, :], ACT.Tanh, scale=0.5).then_inc(tanh_out, 1)
            turned(2)
            g_part(0)
            act.wait_ge(wvo_made, 1)
            act.activation(wvo[:].rearrange("p c n -> p (c n)"), psum[:, BANK_WVO, :], ACT.Copy).then_inc(wvo_ready, 1)
            xn_chunk(1)
            act.wait_ge(trig_in, 1)
            act.activation(s4d[:, 10, 0:HN], s4d[:, 8, 0:HN], ACT.Tanh, scale=0.5)
            act.activation(s4d[:, 11, 0:HN], s4d[:, 9, 0:HN], ACT.Sin)
            act.activation(s4d[:, 12, 0:HN], s4d[:, 9, 0:HN], ACT.Sin, scale=0.5).then_inc(trig_out, 1)
            v_part(0)
            act.wait_ge(scales_turned, 1)
            act.activation(scales[:], psum[:, BANK_SCALES, 0:2 * M], ACT.Copy).then_inc(scales_ready, 1)

            def normalise(n, k, source):
                b, t = tile_of[k]
                act.wait_ge(shift_ready[n], k + 1 if n == 1 else 2 * b + t + 1)
                act.activation(h_rows[:, k % T, :], source[:, k, :], ACT.Identity, scale=rstd[:, n, k:k + 1],
                               bias=neg_mean_rstd[:, n, k:k + 1]).then_inc(h_ready[t // 2], 1)

            def exp_scores(k):
                W = P * (k % T + 1)
                act.wait_ge(max_ready, k + 1)
                if k >= 2:
                    act.wait_ge(probs_turned, k - 1)
                act.activation(probs[:, k % 2, 0:W], psum[:, BANK_S[k % 2], 0:W], ACT.Exp,
                               bias=neg_max[:, k:k + 1], accum_out=row_sum[:, k:k + 1]).then_inc(probs_ready, 1)

            def copy_probs(k):
                W = P * (k % T + 1)
                act.wait_ge(probs_turned, k + 1)
                if k >= 2:
                    act.wait_ge(attn_made, k - 1)
                act.activation(probs_cols[:, k % 2, 0:W], psum[:, BANK_PT[k % 2], 0:W],
                               ACT.Copy).then_inc(probs_cols_ready, 1)

            def copy_h(n):
                for c in range(C):
                    act.wait_ge(h_turned, C * n + c + 1)
                    act.activation(h_head[:, c, :], psum[:, BANK_H[c], :], ACT.Copy).then_inc(h_head_ready, 1)

            exp_scores(0)
            g_part(1)
            exp_scores(1)
            copy_probs(0)
            v_part(1)
            for k in range(2, K):
                exp_scores(k)
                copy_probs(k - 1)
                if k >= 6:
                    normalise(1, 2 * (k - 6), x1)
                    normalise(1, 2 * (k - 6) + 1, x1)
            copy_probs(K - 1)
            copy_h(0)
            act.activation(silu_table[:], params[:, 0:1], ACT.Silu)

            def gate(n, m):
                act.wait_ge(gate_made, M * n + m + 1)
                act.activation(gated[:, m % 2, :], psum[:, BANK_GATE[m % 2], :], ACT.Silu,
                               scale=gate_scales[:, m:m + 1]).then_inc(gated_ready, 1)

            for n in range(2 * B):
                if n >= 1:
                    copy_h(n)
                gate(n, 0)
                for m in range(M):
                    if m + 1 < M:
                        gate(n, m + 1)
                    act.wait_ge(fused_ready, M * n + m + 1)
                    act.activation(f_head[:, m, :], fused[:, m % FUSED, :], ACT.Copy).then_inc(f_head_ready, 1)
                    if n == 0 and m in (1, 2):
                        for k in range(T + 2 * (m - 1), T + 2 * m):
                            normalise(1, k, x1)
                    if n == 1 and m == 2:
                        for t in range(T):
                            act.wait_ge(shift_ready[2], t + 1)
                            act.activation(x_lag[:, t, :], x2[:, t, :], ACT.Identity, scale=rstd[:, 2, t:t + 1],
                                           bias=neg_mean_rstd[:, 2, t:t + 1]).then_inc(z2_ready, 1)
                    if n in (1, 2) and m == 3:
                        for k in range(T * (n - 1), T * (n - 1) + 2):
                            normalise(3, k, x3)

        @block.vector
        def _(dve):
            count = [0]

            def step(ins):
                count[0] += 1
                ins.then_inc(dve_step, 1)
                dve.wait_ge(dve_step, count[0])

            def mark(ins):
                count[0] += 1
                ins.then_inc(dve_step, 1)

            def settle():
                dve.wait_ge(dve_step, count[0])

            def tile_stats(n, tiles, source):
                for k in tiles:
                    mark(dve.bn_stats(stats[:, n, k, :], source[:, k, :]))
                settle()
                for k in tiles:
                    dve.bn_aggr(mean_var[:, n, k, :], stats[:, n, k, :]).then_inc(stats_ready[n], 1)

            def normalise(tiles):
                for k in tiles:
                    dve.wait_ge(rstd_ready[0], k + 1)
                    dve.tensor_scalar(normed[:, k, :], x_in[:, k, :], mean_var[:, 0, k, 0:1], rstd[:, 0, k:k + 1],
                                      ALU.subtract, ALU.mult).then_inc(z_ready, 1)

            def first_stats(b):
                for k in range(T * b, T * b + T, 2):
                    dve.wait_ge(x_loaded[k // 2], 16)
                    tile_stats(0, [k, k + 1], x_in)

            first_stats(0)
            normalise(range(T))
            dve.wait_ge(params_turned, 1)
            dve.tensor_copy(params[:], psum[:, BANK_PARAMS, 0:4 * C]).then_inc(params_ready, 1)

            def xn_chunk(b):
                dve.wait_ge(params_ready, 1)
                dve.wait_ge(z_turned, C * b + 2)
                dve.tensor_scalar(xn_cols[:, b, 1, :], psum[:, BANK_Z[b][1], :], gammas[:, 1:2], betas[:, 1:2],
                                  ALU.mult, ALU.add).then_inc(xn_by_dve, 1)

            def g_chunk(b):
                dve.wait_ge(g_made, C * b + 2)
                dve.tensor_scalar(g_cols[:, b, 1, :], psum[:, BANK_G[b][1], :], float(KEY) ** -0.5, None,
                                  ALU.mult).then_inc(g_by_dve, 1)

            def v_half(b):
                dve.wait_ge(v_made, 2 * b + 2)
                dve.tensor_copy(v_rows[:, b, 2:4, :].rearrange("p t n -> p (t n)"),
                                psum[:, BANK_V[b][1], :]).then_inc(v_by_dve, 1)

            W2 = HN + C
            st = lambda n, w=HN: s4d[:, n, 0:w]

            def exp_reduce():
                dve.wait_ge(a_loaded, 32)
                dve.wait_ge(params_ready, 1)
                dve.tensor_copy(e_in[:, 0:HN], s4d_in[:, 0, :])
                step(dve.tensor_copy(e_in[:, HN:W2], log_dts))
                step(dve.tensor_scalar(st(0, W2), e_in[:], LOG2E, ROUND, ALU.mult, ALU.add))
                step(dve.tensor_scalar(st(0, W2), st(0, W2), -ROUND, None, ALU.add))
                step(dve.scalar_tensor_tensor(out=st(1, W2), in0=st(0, W2), scalar=-LN2_HI, in1=e_in[:], op0=ALU.mult, op1=ALU.add))
                step(dve.scalar_tensor_tensor(out=st(2, W2), in0=st(0, W2), scalar=-LN2_LO, in1=st(1, W2), op0=ALU.mult, op1=ALU.add))
                step(dve.tensor_scalar(st(4, W2), st(0, W2), -127.0, 128.0, ALU.max, ALU.min))
                dve.tensor_scalar(two_k[:], st(4, W2), 127.0, 2.0**23, ALU.add, ALU.mult).then_inc(tanh_in, 1)

            def exp_finish():
                dve.wait_ge(tanh_in, 1)
                dve.wait_ge(tanh_out, 1)
                step(dve.tensor_scalar(st(4, W2), st(3, W2), -1.0, 1.0, ALU.mult, ALU.add))
                step(dve.reciprocal(st(5, W2), st(4, W2)))
                step(dve.scalar_tensor_tensor(out=st(6, W2), in0=st(3, W2), scalar=1.0, in1=st(5, W2), op0=ALU.add, op1=ALU.mult))
                step(dve.tensor_tensor(st(7, W2), st(6, W2), two_k[:].bitcast(F32), ALU.mult))
                for c in range(C):
                    dt = s4d[:, 7, HN + c:HN + c + 1]
                    cs = slice(N * c, N * c + N)
                    dve.tensor_scalar(s4d[:, 8, cs], s4d[:, 7, cs], dt, -1.0, ALU.mult, ALU.mult)
                    step(dve.tensor_scalar(s4d[:, 13, cs], s4d_in[:, 1, cs], dt, None, ALU.mult))

            def reduce_angle():
                step(dve.tensor_scalar(st(14), st(13), 1.0 / (2.0 * np.pi), ROUND, ALU.mult, ALU.add))
                step(dve.tensor_scalar(st(14), st(14), -ROUND, None, ALU.add))
                for part in TWO_PI:
                    step(dve.scalar_tensor_tensor(out=st(13), in0=st(14), scalar=-part, in1=st(13), op0=ALU.mult, op1=ALU.add))
                dve.tensor_scalar(st(9), st(13), -PI_BELOW, PI_BELOW, ALU.max, ALU.min).then_inc(trig_in, 1)

            def magnitude():
                w, a = s4d_in[:, 1, :], st(7)
                mark(dve.tensor_tensor(st(27), a, a, ALU.mult))
                mark(dve.tensor_tensor(st(28), w, w, ALU.mult))
                dve.wait_ge(trig_out, 1)
                step(dve.tensor_scalar(st(15), st(10), -1.0, 1.0, ALU.mult, ALU.add))
                mark(dve.reciprocal(st(16), st(15)))
                step(dve.tensor_tensor(st(28), st(27), st(28), ALU.add))
                dve.reciprocal(st(29), st(28))
                dve.scalar_tensor_tensor(out=st(17), in0=st(10), scalar=2.0, in1=st(16), op0=ALU.mult,
                                         op1=ALU.mult).then_inc(magnitude_ready, 1)

            def weight_square(w):
                dve.wait_ge(w_loaded[w], 16)
                mark(dve.tensor_tensor_reduce(square[w][:], flat(raws[w]), flat(raws[w]), 1.0, 0.0, ALU.mult, ALU.max, max_square[:, w:w + 1]))

            def weight_grid(w):
                step(dve.tensor_scalar(grid[w][:].bitcast(U32), flat(raws[w]).bitcast(U32), 0x7F800000, None, ALU.bitwise_and))
                dve.tensor_scalar(grid[w][:], grid[w][:], 2.0**-6, 1.5 * 2.0**20, ALU.max, ALU.mult).then_inc(grid_ready, 1)

            def mark_beyond():
                dve.wait_ge(grid_ready, 3)
                step(dve.tensor_reduce(max_square[:, 3:4], max_square[:, 0:3], AX_X, ALU.max))
                dve.tensor_scalar(beyond[:, 0:1], max_square[:, 3:4], FP8_LARGEST**2, None, ALU.is_gt).then_inc(squares_ready, 1)

            def read_norms():
                dve.wait_ge(norms_made, 1)
                mark(dve.tensor_scalar(bound[:, 0, :], psum[:, BANK_NORMS, 0:M], 2.26, 5e-4, ALU.mult, ALU.add))
                mark(dve.tensor_scalar(bound[:, 1, :], psum[:, BANK_NORMS, M:2 * M], 2.26, 5e-4, ALU.mult, ALU.add))
                dve.tensor_scalar(beyond[:, 1:2], psum[:, BANK_NORMS, 2 * M:2 * M + 1], 0.0, 3e38, ALU.is_gt,
                                  ALU.mult).then_inc(norms_read, 1)

            def bound_gate_up():
                dve.wait_ge(norms_read, 1)
                mark(dve.tensor_scalar(beyond[:, 2:3], beyond[:, 1:2], 3e38, None, ALU.mult))
                dve.wait_ge(scales_ready, 1)
                mark(dve.tensor_tensor(bound[:, 2, :], gate_scales, up_scales, ALU.mult))
                settle()
                mark(dve.tensor_tensor(bound[:, 2, :], bound[:, 2, :], bound[:, 2, :], ALU.mult))
                mark(dve.tensor_tensor(bound[:, 1, :], bound[:, 1, :], bound[:, 0, :], ALU.mult))
                mark(dve.tensor_tensor(beyond[:, 3:4], beyond[:, 2:3], beyond[:, 2:3], ALU.subtract))
                settle()
                dve.scalar_tensor_tensor(out=bound[:, 3, :], in0=bound[:, 1, :], scalar=65536.0, in1=bound[:, 2, :],
                                         op0=ALU.mult, op1=ALU.mult).then_inc(bound_squared, 1)
                dve.wait_ge(down_scale_loaded, 16)
                dve.tensor_scalar(down_scale_all[:], down_scale_all[:], beyond[:, 3:4], None, ALU.add)

            def fit_powers():
                dve.wait_ge(bound_ready, 1)
                step(dve.tensor_scalar(bound[:, 5, :].bitcast(U32), bound[:, 4, :].bitcast(U32), 0x7F800000, None, ALU.bitwise_and))
                step(dve.tensor_scalar(bound[:, 6, :], bound[:, 5, :], 2.0**-80, 2.0**-14, ALU.max, ALU.mult))
                step(dve.reciprocal(bound[:, 7, :], bound[:, 6, :]))
                dve.tensor_tensor(up_scales_fit[:], up_scales, bound[:, 7, :], ALU.mult).then_inc(fit_ready, 1)

            def h_tails(n):
                for c in range(C):
                    dve.wait_ge(h_head_ready, C * n + c + 1)
                    dve.tensor_tensor(h_tail[:, c, :], psum[:, BANK_H[c], :], h_head[:, c, :],
                                      ALU.subtract).then_inc(h_tail_ready, 1)

            def row_max(k):
                dve.wait_ge(scores_made, k + 1)
                dve.tensor_reduce(neg_max[:, k:k + 1], psum[:, BANK_S[k % 2], 0:P * (k % T + 1)], AX_X, ALU.max,
                                  negate=True).then_inc(max_ready, 1)

            def attention_out(k):
                dve.wait_ge(probs_ready, k + 1)
                step(dve.reciprocal(inv_sum[:, k:k + 1], row_sum[:, k:k + 1]))
                dve.wait_ge(attn_made, k + 1)
                dve.wait_ge(x_plus_ready, k + 1)
                dve.scalar_tensor_tensor(out=x1[:, k, :], in0=psum[:, BANK_O[k % 2], 0:H], scalar=inv_sum[:, k:k + 1],
                                         in1=x_plus[:, k, :], op0=ALU.mult, op1=ALU.add).then_inc(x1_ready, 1)
                dve.wait_ge(x1_ready, k + 1)
                tile_stats(1, [k], x1)

            xn_chunk(0)
            exp_reduce()
            first_stats(1)
            exp_finish()
            normalise(range(T, K))
            g_chunk(0)
            reduce_angle()
            weight_square(0)
            xn_chunk(1)
            magnitude()
            weight_grid(0)
            v_half(0)
            row_max(0)
            weight_square(1)
            g_chunk(1)
            row_max(1)
            weight_grid(1)
            weight_square(2)
            v_half(1)
            for k in range(2, K):
                row_max(k)
                if k == 3:
                    weight_grid(2)
                if k == 4:
                    mark_beyond()
                if k == 6:
                    read_norms()
                if k == 7:
                    bound_gate_up()
                attention_out(k - 2)
            attention_out(K - 2)
            h_tails(0)
            fit_powers()
            attention_out(K - 1)

            def ffn_scale(j):
                k, t = j % K, j % T
                dve.wait_ge(down_made, j // 2 + 1)
                dve.tensor_tensor(scaled_down[:, k, :], psum[:, BANK_DOWN[t // 2], H * (t % 2):H * (t % 2) + H],
                                  down_scale_all[:], ALU.mult).then_inc(down_read, 1)

            def x2_stats(tiles):
                b, t = tile_of[tiles[0]]
                dve.wait_ge(x2_by_pool, 3 * b + (1 if t == 0 else 3))
                dve.wait_ge(x2_by_dve, b + 1)
                tile_stats(2, tiles, x2)

            def x3_stats(tiles):
                dve.wait_ge(x3_ready, tiles[-1] + 1)
                tile_stats(3, tiles, x3)

            def add_x1(k):
                dve.wait_ge(down_read, k + 1)
                dve.tensor_tensor(x2[:, k, :], scaled_down[:, k, :], x1[:, k, :], ALU.add).then_inc(x2_by_dve, 1)

            def s4d_begin(tiles):
                dve.wait_ge(taps_loaded, 16)
                for k in tiles:
                    mark(dve.scalar_tensor_tensor(out=normed[:, k, :], in0=x2[:, k, :], scalar=mean_var[:, 2, k, 0:1],
                                                  in1=taps_all[:, 0, :], op0=ALU.subtract, op1=ALU.mult))

            def s4d_end(tiles):
                settle()
                for k in tiles:
                    b, t = tile_of[k]
                    dve.wait_ge(rstd_ready[2], k + 1)
                    if b:
                        dve.wait_ge(lag_ready, t + 1)
                    dve.scalar_tensor_tensor(out=x3[:, k, :], in0=normed[:, k, :], scalar=rstd[:, 2, k:k + 1],
                                             in1=x2_lag[:, t, :] if b else x2[:, k, :], op0=ALU.mult,
                                             op1=ALU.add).then_inc(x3_ready, 1)

            def norm_rows(k):
                dve.wait_ge(rstd_ready[3], k + 1)
                dve.tensor_scalar(h_rows[:, k % T, :], x3[:, k, :], mean_var[:, 3, k, 0:1], rstd[:, 3, k:k + 1],
                                  ALU.subtract, ALU.mult).then_inc(h_ready[1], 1)

            def fuse(n, m):
                i = M * n + m
                dve.wait_ge(gated_ready, i + 1)
                dve.wait_ge(up_made, i + 1)
                if i >= FUSED and (m - FUSED) % M in POOL_TAILS:
                    dve.wait_ge(f_tail_by_pool, len(POOL_TAILS) * ((i - FUSED) // M) + POOL_TAILS.index((m - FUSED) % M) + 1)
                dve.scalar_tensor_tensor(out=fused[:, m % FUSED, :], in0=psum[:, BANK_UP[m % 2], :],
                                         scalar=up_scales_fit[:, m:m + 1], in1=gated[:, m % 2, :],
                                         op0=ALU.mult, op1=ALU.mult).then_inc(fused_ready, 1)

            def tail(n, m):
                dve.wait_ge(f_head_ready, M * n + m + 1)
                dve.tensor_tensor(f_tail[:, m, :], fused[:, m % FUSED, :], f_head[:, m, :],
                                  ALU.subtract).then_inc(f_tail_by_dve, 1)

            for n in range(2 * B):
                if n >= 1:
                    h_tails(n)
                    for j in range(T * (n - 1), T * n):
                        ffn_scale(j)
                if n in (1, 2):
                    tiles = list(range(T * (n - 1), T * n))
                    first, second = tiles[:2], tiles[2:]
                    add_x1(tiles[1])
                    x2_stats(first)
                    fuse(n, 0)
                    x2_stats(second)
                    fuse(n, 1)
                    tail(n, 0)
                    s4d_begin(first)
                    s4d_end(first)
                    fuse(n, 2)
                    x3_stats(first)
                    s4d_begin(second)
                    fuse(n, 3)
                    s4d_end(second)
                    tail(n, 2)
                    x3_stats(second)
                    fuse(n, 4)
                    fuse(n, 5)
                    for k in second:
                        norm_rows(k)
                    tail(n, 5)
                else:
                    for m in range(M):
                        fuse(n, m)
                        if m in DVE_TAILS:
                            tail(n, m)
            def add_x3(t):
                k = T + t
                dve.wait_ge(down_read, K + k + 1)
                dve.tensor_tensor(x4[:, k, :], scaled_down[:, k, :], x3[:, k, :], ALU.add).then_inc(x4_by_dve, 1)

            for t in (1, 3):
                ffn_scale(3 * T + t - 1)
                ffn_scale(3 * T + t)
                add_x3(t)

        @block.tensor
        def _(pe):
            def column(bank, start, width):
                return psum[:, bank, start:start + width]

            pe.wait_ge(ident_ready, 1)
            for n in range(WARM_UP):
                pe.transpose(column(BANK_NORMS, 0, P), ident[:], ident[:])

            def turn_w(w, loaded):
                pe.wait_ge(loaded, 16)
                for kc in range(C):
                    for c in range(C):
                        last = pe.transpose(column(BANK_WT[w], kc * H + c * P, P),
                                            qkv_sb[:, c, w * KEY + kc * P:w * KEY + kc * P + P], ident[:])
                last.then_inc(w_turned_pe, 1)

            def fold(bank, left, right):
                for c in range(C):
                    for kc in range(C):
                        last = pe.matmul(column(bank, c * H, H), w_turned[:, left, kc, c * P:c * P + P], right(kc),
                                         start=(kc == 0), stop=(kc == C - 1))
                return last

            def turn_z(b):
                for t in range(T):
                    pe.wait_ge(z_ready, T * b + t + 1)
                    for c in range(C):
                        turned = pe.transpose(column(BANK_Z[b][c], t * P, P), normed[:, T * b + t, c * P:c * P + P], ident[:])
                        if t == T - 1:
                            turned.then_inc(z_turned, 1)

            def make_g(b):
                pe.wait_ge(xn_by_act, b + 1)
                pe.wait_ge(xn_by_dve, b + 1)
                for j in range(C):
                    for c in range(C):
                        last = pe.matmul(column(BANK_G[b][j], 0, S), wqk[:, c, j * P:j * P + P], xn_cols[:, b, c, :],
                                         start=(c == 0), stop=(c == C - 1))
                    last.then_inc(g_made, 1)

            def make_v(b):
                for t in range(T):
                    for c in range(C):
                        last = pe.matmul(column(BANK_V[b][t // 2], H * (t % 2), H), xn_cols[:, b, c, t * P:t * P + P],
                                         wvo[:, c, :], start=(c == 0), stop=(c == C - 1))
                    if t % 2:
                        last.then_inc(v_made, 1)

            turn_w(0, q_loaded)
            turn_w(1, k_loaded)
            pe.wait_ge(params_loaded, 64)
            pe.transpose(column(BANK_PARAMS, 0, 4 * C), param_rows[:], ident[0:4 * C, 0:4 * C]).then_inc(params_turned, 1)
            turn_z(0)
            pe.wait_ge(w_turned_ready, 2)
            fold(BANK_WQK, 0, lambda kc: w_turned[:, 1, kc, :]).then_inc(wqk_made, 1)
            turn_w(2, v_loaded)
            pe.wait_ge(wqk_ready, 1)
            pe.wait_ge(params_ready, 1)
            make_g(0)
            pe.wait_ge(w_turned_ready, 3)
            pe.wait_ge(wo_loaded, 16)
            fold(BANK_WVO, 2, lambda kc: wo_sb[:, kc, :]).then_inc(wvo_made, 1)
            def scores(k):
                b, i = tile_of[k]
                if k == 0:
                    pe.wait_ge(consts_ready, 1)
                    pe.wait_ge(g_by_act, 1)
                    pe.wait_ge(g_by_dve, 1)
                if k == T:
                    pe.wait_ge(g_by_act, 2)
                    pe.wait_ge(g_by_dve, 2)
                if k >= 2:
                    pe.wait_ge(probs_ready, k - 1)
                W = P * (i + 1)
                for j in range(C):
                    pe.matmul(column(BANK_S[k % 2], 0, W), g_cols[:, b, j, i * P:i * P + P], xn_cols[:, b, j, 0:W],
                              start=(j == 0), stop=(j == C - 1))
                pe.matmul(column(BANK_S[k % 2], i * P, P), ident16[:], mask[:], start=False, stop=True,
                          skip_group_check=True).then_inc(scores_made, 1)

            def turn_probs(k):
                pe.wait_ge(probs_ready, k + 1)
                if k == 0:
                    pe.wait_ge(v_by_act, 1)
                    pe.wait_ge(v_by_dve, 1)
                if k >= 2:
                    pe.wait_ge(probs_cols_ready, k - 1)
                for t in range(k % T + 1):
                    last = pe.transpose(column(BANK_PT[k % 2], t * P, P), probs[:, k % 2, t * P:t * P + P], ident[:])
                last.then_inc(probs_turned, 1)

            def attend(k):
                b, i = tile_of[k]
                pe.wait_ge(probs_cols_ready, k + 1)
                if k == T:
                    pe.wait_ge(v_by_act, 2)
                    pe.wait_ge(v_by_dve, 2)
                if k >= 2:
                    pe.wait_ge(x1_ready, k - 1)
                for t in range(i + 1):
                    last = pe.matmul(column(BANK_O[k % 2], 0, H), probs_cols[:, k % 2, t * P:t * P + P],
                                     v_rows[:, b, t, :], start=(t == 0), stop=(t == i))
                last.then_inc(attn_made, 1)

            def channel_norms():
                pe.wait_ge(squares_ready, 1)
                pe.wait_ge(v_by_dve, 2)
                for w in range(2):
                    for m in range(M):
                        for c in range(C):
                            pe.matmul(column(BANK_NORMS, M * w + m, 1), square[w][:, c * I + m * P:c * I + m * P + P],
                                      ones16[:, 0:1], start=(c == 0), stop=(c == C - 1))
                pe.matmul(column(BANK_NORMS, 2 * M, 1), ones[:], beyond[:, 0:1], start=True,
                          stop=True).then_inc(norms_made, 1)

            def turn_h(n, half, first=False):
                pe.wait_ge(h_ready[half], n * 2 + 2)
                if not first:
                    pe.wait_ge(h_tail_ready, n * C)
                for c in range(C):
                    for t in (2 * half, 2 * half + 1):
                        last = pe.transpose(column(BANK_H[c], t * P, P), h_rows[:, t, c * P:c * P + P], ident[:])
                    if half == 1:
                        last.then_inc(h_turned, 1)

            turn_z(1)
            pe.wait_ge(wvo_ready, 1)
            make_v(0)
            scores(0)
            pe.wait_ge(scales_loaded, 32)
            pe.wait_ge(xn_by_act, 2)
            pe.transpose(column(BANK_SCALES, 0, 2 * M), scale_rows[:], ident[0:2 * M, 0:2 * M]).then_inc(scales_turned, 1)
            make_g(1)
            scores(1)
            turn_probs(0)
            pe.wait_ge(scales_ready, 1)
            make_v(1)
            for k in range(2, K):
                scores(k)
                turn_probs(k - 1)
                if k == 5:
                    channel_norms()
                attend(k - 2)
            turn_probs(K - 1)
            attend(K - 2)
            pe.wait_ge(norms_read, 1)
            turn_h(0, 0, first=True)
            turn_h(0, 1, first=True)
            attend(K - 1)
            pe.wait_ge(gate_up_ready, 2)

            def gate_up(n, m):
                for w, banks, made, read in ((gate16, BANK_GATE, gate_made, gated_ready), (up16, BANK_UP, up_made, fused_ready)):
                    if m >= 2:
                        pe.wait_ge(read, n * M + (m - 1))
                    for part, ready in ((h_head, h_head_ready), (h_tail, h_tail_ready)):
                        for c in range(C):
                            if m == 0 and w is gate16:
                                pe.wait_ge(ready, n * C + (c + 1))
                            last = pe.matmul(column(banks[m % 2], 0, S), w[:, c, m * P:m * P + P], part[:, c, :],
                                             start=(part is h_head and c == 0), stop=(part is h_tail and c == C - 1))
                    last.then_inc(made, 1)

            def down(n, m):
                if m in POOL_TAILS:
                    pe.wait_ge(f_tail_by_pool, n * len(POOL_TAILS) + (POOL_TAILS.index(m) + 1))
                else:
                    pe.wait_ge(f_tail_by_dve, n * len(DVE_TAILS) + (DVE_TAILS.index(m) + 1))
                pe.wait_ge(down_ready, m + 1)
                for t in range(T):
                    for part in (f_head, f_tail):
                        last = pe.matmul(column(BANK_DOWN[t // 2], H * (t % 2), H), part[:, m, t * P:t * P + P],
                                         down16[:, m, :], start=(m == 0 and t % 2 == 0 and part is f_head),
                                         stop=(m == M - 1 and part is f_tail), skip_group_check=True)
                    if m == M - 1 and t % 2:
                        last.then_inc(down_made, 1)

            LAG = 3

            def ffn_pass(n):
                for m in range(M):
                    gate_up(n, m)
                    if m >= LAG:
                        down(n, m - LAG)

            with pe.Fori(0, 2 * B - 1) as n:
                ffn_pass(n)
                turn_h(n + 1, 0)
                down(n, M - 3)
                turn_h(n + 1, 1)
                down(n, M - 2)
                down(n, M - 1)
            ffn_pass(2 * B - 1)
            for m in range(M - LAG, M):
                down(2 * B - 1, m)


_INS = ['x', 'qkv', 'o_proj', 'gamma', 'beta', 'd_param', 'log_dt', 'a_real_log', 'a_imag', 'c_re', 'c_im',
        'gate_w', 'up_w', 'down_w', 'gate_scale', 'up_scale', 'down_scale']


def kernel(L0_attn_a_x, L0_attn_a_qkv, L0_attn_a_o_proj, L0_attn_a_gamma, L0_attn_a_beta, L0_attn_b_D_param,
           L0_attn_b_log_dt, L0_attn_b_A_real_log, L0_attn_b_A_imag, L0_attn_b_C_re, L0_attn_b_C_im, L0_ffn_gate_w,
           L0_ffn_up_w, L0_ffn_down_w, L0_ffn_gate_scale, L0_ffn_up_scale, L0_ffn_down_scale):
    import concourse.bacc as bacc
    from concourse.bass_utils import run_bass_kernel_spmd

    given = (L0_attn_a_x, L0_attn_a_qkv, L0_attn_a_o_proj, L0_attn_a_gamma, L0_attn_a_beta, L0_attn_b_D_param,
             L0_attn_b_log_dt, L0_attn_b_A_real_log, L0_attn_b_A_imag, L0_attn_b_C_re, L0_attn_b_C_im, L0_ffn_gate_w,
             L0_ffn_up_w, L0_ffn_down_w, L0_ffn_gate_scale, L0_ffn_up_scale, L0_ffn_down_scale)
    nc = bacc.Bacc("TRN2", target_bir_lowering=False, num_devices=1)
    arrays, aps = {}, []
    for name, value in zip(_INS, given):
        array = np.ascontiguousarray(value)
        arrays[f"in_{name}"] = array
        aps.append(nc.dram_tensor(f"in_{name}", array.shape, mybir.dt.from_np(array.dtype), kind="ExternalInput").ap())
    out = nc.dram_tensor("out", arrays["in_x"].shape, F32, kind="ExternalOutput").ap()
    hybrid_layer(nc, *aps, out)
    result = run_bass_kernel_spmd(nc, [arrays], core_ids=[0])
    return result.results[0]["out"]
```
